# Optimizing a Trainium2 kernel written in Bass

```python
import numpy as np
import jax
import jax.numpy as jnp

def _softmax(x, axis=-1):
    return jax.nn.softmax(x, axis=axis)

def _gelu(x):
    return jax.nn.gelu(x, approximate=True)

def _silu(x):
    return jax.nn.silu(x)

def _sigmoid(x):
    return jax.nn.sigmoid(x)

def _layernorm(x, axis=-1, eps=1e-05):
    m = jnp.mean(x, axis=axis, keepdims=True)
    v = jnp.var(x, axis=axis, keepdims=True)
    return (x - m) / jnp.sqrt(v + eps)

def _scatter_add(tgt, idx, src, axis=0):
    return tgt.at[idx].add(src)

def _segment_sum(src, seg, n):
    return jax.ops.segment_sum(src, seg, n)
kernel_name = 'mk_cond_resid_d4_seqx_r4_53b054'

def setup_inputs(seed: int=0):
    np.random.seed(seed)
    _w = jnp.asarray

    def _rec_inputs():
        import jax
        import jax.numpy as jnp
        _rk = jax.random.key(seed)
        x = 7.22e-05 + 1 * jax.random.normal(jax.random.fold_in(_rk, 1), (8, 256, 1024), jnp.float32)
        _lenS = 256 - jax.random.randint(jax.random.fold_in(_rk, 7), (8,), 0, max(1, 256 // 4) + 1, jnp.int32)
        _lenS2 = 256 - jax.random.randint(jax.random.fold_in(_rk, 8), (8,), 0, max(1, 256 // 4) + 1, jnp.int32)
        condB_coeff = 0.00219231 + 0.0100837 * jax.random.normal(jax.random.fold_in(_rk, 11), (8,), jnp.float32)
        condB_codebook = -0.0625 + 0.715345 * jax.random.normal(jax.random.fold_in(_rk, 13), (8,), jnp.float32)
        itok_B_0_23 = jax.random.randint(jax.random.fold_in(_rk, 14), (8,), 0, 24, jnp.int32)
        itok_B_4_50 = jax.random.randint(jax.random.fold_in(_rk, 15), (8,), 4, 51, jnp.int32)
        _validS = jnp.arange(256)[None, :] < _lenS[:, None]
        _validS2 = jnp.arange(256)[None, :] < _lenS2[:, None]
        _causal = jnp.tril(jnp.ones((256, 256), dtype=bool))
        mask_Bx4096x4096_ik1 = jnp.where(jnp.ones((8, 1024, 1024), dtype=bool), 1, 0).astype(jnp.int32)
        return (x, condB_coeff, condB_codebook, itok_B_0_23, itok_B_4_50, mask_Bx4096x4096_ik1)
    x, condB_coeff, condB_codebook, itok_B_0_23, itok_B_4_50, mask_Bx4096x4096_ik1 = _rec_inputs()

    def _L0_cond_setup():
        import jax, jax.numpy as jnp
        import numpy as np
        B, S, D_IN, D_OUT = (4, 128, 1024, 1024)
        key = jax.random.key(seed)
        k1, k2, k3, k4, k5 = jax.random.split(key, 5)
        hidden_states = jax.random.normal(k1, (B, S, D_IN), dtype=jnp.float32)
        W = jax.random.normal(k2, (D_OUT, D_IN), dtype=jnp.float32) * 0.02
        b = jax.random.normal(k3, (D_OUT,), dtype=jnp.float32) * 0.02
        coeff = jax.random.normal(k4, (B,), dtype=jnp.float32) * 0.01
        mask = jax.random.randint(k5, (B, D_IN, D_OUT), 0, 2, dtype=jnp.int32)
        return {'hidden_states': hidden_states, 'W': W, 'b': b, 'coeff': coeff, 'mask': mask}
    _L0_cond_all = _L0_cond_setup()
    _L0_cond_in = {k: v for k, v in _L0_cond_all.items() if k in ('W', 'b')}
    del _L0_cond_all

    def _L1_cond_setup():
        import jax, jax.numpy as jnp
        import numpy as np
        GROUP = 128
        LORA_ALPHA = 32.0
        LORA_RANK = 64
        key = jax.random.key(seed)
        k1, k2, k3, k4 = jax.random.split(key, 4)
        O, I = (1024, 1024)
        x = jax.random.normal(k1, (4, 512, I), dtype=jnp.float32)
        weight = jax.random.normal(k2, (O, I), dtype=jnp.float32) * 0.02
        wg = weight.reshape(O, I // GROUP, GROUP)
        scale_log = jnp.log(jnp.clip(jnp.max(jnp.abs(wg), axis=2, keepdims=True), 1e-05))
        codebook = jnp.array([-1.0, -0.25, 0.0, 1.0], dtype=jnp.float32)
        lora_A = jax.random.normal(k3, (LORA_RANK, I), dtype=jnp.float32) * 0.02
        lora_B = jax.random.normal(k4, (O, LORA_RANK), dtype=jnp.float32) * 0.02
        return {'x': x, 'weight': weight, 'scale_log': scale_log, 'codebook': codebook, 'lora_A': lora_A, 'lora_B': lora_B}
    _L1_cond_all = _L1_cond_setup()
    _L1_cond_in = {k: v for k, v in _L1_cond_all.items() if k in ('weight', 'scale_log', 'lora_A', 'lora_B')}
    del _L1_cond_all

    def _L2_cond_setup():
        import jax, jax.numpy as jnp
        import numpy as np
        R = 16
        ALPHA = 32
        SCALING = ALPHA / R
        SLOTS = 32
        IN_F = 1024
        OUT_F = 1024
        B, T = (8, 256)
        key = jax.random.key(seed)
        k1, k2, k3, k4, k5, k6 = jax.random.split(key, 6)
        x = jax.random.normal(k1, (B, T, IN_F), dtype=jnp.float32)
        adapter_mapping = jax.random.randint(k2, (B,), 0, SLOTS, dtype=jnp.int32)
        W = jax.random.normal(k3, (OUT_F, IN_F), dtype=jnp.float32) * 0.02
        b = jax.random.normal(k4, (OUT_F,), dtype=jnp.float32) * 0.02
        lora_As = jax.random.normal(k5, (SLOTS, IN_F, R), dtype=jnp.float32) * 0.02
        lora_Bs = jax.random.normal(k6, (SLOTS, R, OUT_F), dtype=jnp.float32) * 0.02
        return {'x': x, 'adapter_mapping': adapter_mapping, 'W': W, 'b': b, 'lora_As': lora_As, 'lora_Bs': lora_Bs}
    _L2_cond_all = _L2_cond_setup()
    _L2_cond_in = {k: v for k, v in _L2_cond_all.items() if k in ('W', 'b', 'lora_As', 'lora_Bs')}
    del _L2_cond_all

    def _L3_cond_setup():
        import jax, jax.numpy as jnp
        import numpy as np
        RANK = 16
        ALPHA = 16.0
        SCALING = ALPHA / RANK
        key = jax.random.key(seed)
        k1, k2, k3, k4 = jax.random.split(key, 4)
        batch, n_tok, d_in, d_out, n_adapters, rank = (8, 512, 1024, 1024, 64, RANK)
        x = jax.random.normal(k1, (batch, n_tok, d_in), dtype=jnp.float32)
        A = jax.random.normal(k2, (n_adapters, d_out, rank), dtype=jnp.float32) * 0.02
        B = jax.random.normal(k3, (n_adapters, rank, d_in), dtype=jnp.float32)
        adapter_ids = jax.random.randint(k4, (batch,), 0, n_adapters, dtype=jnp.int32)
        return {'x': x, 'A': A, 'B': B, 'adapter_ids': adapter_ids}
    _L3_cond_all = _L3_cond_setup()
    _L3_cond_in = {k: v for k, v in _L3_cond_all.items() if k in ('A', 'B')}
    del _L3_cond_all
    return {'x': x, 'condB_coeff': condB_coeff, 'condB_codebook': condB_codebook, 'itok_B_0_23': itok_B_0_23, 'itok_B_4_50': itok_B_4_50, 'mask_Bx4096x4096_ik1': mask_Bx4096x4096_ik1, 'L0_cond_W': _L0_cond_in['W'], 'L0_cond_b': _L0_cond_in['b'], 'L1_cond_weight': _L1_cond_in['weight'], 'L1_cond_scale_log': _L1_cond_in['scale_log'], 'L1_cond_lora_A': _L1_cond_in['lora_A'], 'L1_cond_lora_B': _L1_cond_in['lora_B'], 'L2_cond_W': _L2_cond_in['W'], 'L2_cond_b': _L2_cond_in['b'], 'L2_cond_lora_As': _L2_cond_in['lora_As'], 'L2_cond_lora_Bs': _L2_cond_in['lora_Bs'], 'L3_cond_A': _L3_cond_in['A'], 'L3_cond_B': _L3_cond_in['B']}

def reference(x, condB_coeff, condB_codebook, itok_B_0_23, itok_B_4_50, mask_Bx4096x4096_ik1, L0_cond_W, L0_cond_b, L1_cond_weight, L1_cond_scale_log, L1_cond_lora_A, L1_cond_lora_B, L2_cond_W, L2_cond_b, L2_cond_lora_As, L2_cond_lora_Bs, L3_cond_A, L3_cond_B):
    import jax
    import jax.numpy as jnp

    def _L0_cond_ref(hidden_states, W, b, coeff, mask):
        import jax, jax.numpy as jnp
        import numpy as np
        B, S, D_IN, D_OUT = (4, 128, 1024, 1024)
        output = jnp.einsum('bsi,oi->bso', hidden_states, W) + b
        sign = (2 * mask - 1).astype(hidden_states.dtype)
        diff = jnp.einsum('bsi,bio->bso', hidden_states, sign)
        return output + diff * coeff[:, None, None]

    def _L1_cond_ref(x, weight, scale_log, codebook, lora_A, lora_B):
        import jax, jax.numpy as jnp
        import numpy as np
        GROUP = 128
        LORA_ALPHA = 32.0
        LORA_RANK = 64
        O, I = weight.shape
        lora_delta = lora_B @ lora_A * (LORA_ALPHA / LORA_RANK)
        cb = codebook / jnp.clip(jnp.max(jnp.abs(codebook)), 1e-08)
        scale = jnp.exp(scale_log)
        wg = (weight + lora_delta).reshape(O, I // GROUP, GROUP)
        normalized = wg / scale
        thresholds = (cb[:-1] + cb[1:]) * 0.5
        idx = jnp.searchsorted(thresholds, normalized, side='left')
        quantized = cb[idx]
        w = jax.lax.stop_gradient(quantized - normalized) + normalized
        w_q = (w * scale).reshape(O, I)
        w_eff = w_q + lora_delta
        return x @ w_eff.T

    def _L2_cond_ref(x, adapter_mapping, W, b, lora_As, lora_Bs):
        import jax, jax.numpy as jnp
        import numpy as np
        R = 16
        ALPHA = 32
        SCALING = ALPHA / R
        SLOTS = 32
        IN_F = 1024
        OUT_F = 1024
        B, T = (8, 256)
        base_out = jnp.einsum('bti,oi->bto', x, W) + b
        A = lora_As[adapter_mapping]
        Bm = lora_Bs[adapter_mapping]
        lora_h = jnp.einsum('bti,bir->btr', x, A)
        lora_out = jnp.einsum('btr,bro->bto', lora_h, Bm)
        return base_out + lora_out * SCALING

    def _L3_cond_ref(x, A, B, adapter_ids):
        import jax, jax.numpy as jnp
        import numpy as np
        RANK = 16
        ALPHA = 16.0
        SCALING = ALPHA / RANK
        B_req = B[adapter_ids]
        A_req = A[adapter_ids]
        Bx = jnp.einsum('bni,bri->bnr', x, B_req)
        out = jnp.einsum('bnr,bor->bno', Bx, A_req)
        return out * SCALING
    x = x + _L0_cond_ref(x, L0_cond_W, L0_cond_b, condB_coeff, mask_Bx4096x4096_ik1)
    x = x + _L1_cond_ref(x, L1_cond_weight, L1_cond_scale_log, condB_codebook, L1_cond_lora_A, L1_cond_lora_B)
    x = x + _L2_cond_ref(x, itok_B_0_23, L2_cond_W, L2_cond_b, L2_cond_lora_As, L2_cond_lora_Bs)
    x = x + _L3_cond_ref(x, L3_cond_A, L3_cond_B, itok_B_4_50)
    return x

_drawn_inputs = setup_inputs


def setup_inputs(seed=0):
    import zlib

    import numpy as np

    out = dict(_drawn_inputs(seed))
    spreads = {}
    factors = {'L0_cond_b': 5.551, 'L2_cond_b': 8.0}
    for name, (base, spread) in spreads.items():
        noise = np.random.default_rng([zlib.crc32(name.encode()), seed]).standard_normal(out[name].shape)
        drawn = base * np.exp(spread * noise) if base else spread * noise
        out[name] = jnp.asarray(drawn.astype(out[name].dtype))
    for name, factor in factors.items():
        out[name] = (out[name] * factor).astype(out[name].dtype)
    return out
```

```python
import concourse.bass as bass
from concourse import mybir
from contextlib import ExitStack

F32 = mybir.dt.float32
F32R = mybir.dt.float32r
I32 = mybir.dt.int32
ALU = mybir.AluOpType
ACT = mybir.ActivationFunctionType
AXX = mybir.AxisListType.X


class Order:

    def __init__(self, engine, sem):
        self.engine, self.sem, self.base, self.n = engine, sem, 0, 0

    def did(self, ins):
        ins.then_inc(self.sem, 1)
        self.n += 1

    def wait(self):
        self.engine.wait_ge(self.sem, self.base + self.n)

    def rebase(self, base):
        self.base, self.n = base, 0


def cond_resid_chain(nc, x, coeff, codebook, tok2, tok3, mask, w0, b0, w1, scale_log, lora_a, lora_b,
                     w2, b2, a2, bb2, a3, bb3, out):
    NB, T, D = x.shape
    P = 128
    KT = D // P
    R = a2.shape[2]
    RL = lora_a.shape[0]
    NBR = NB * R
    TT = T // P
    HALF = D // 2
    HT = KT // 2
    NCB = codebook.shape[0]
    NTH = NCB - 1
    EXT = D + 2 * NBR
    G = KT
    MR = 4
    L1_SCALE, L2_SCALE = 0.5, 2.0

    w2_rows = w2.rearrange("(t p) n -> t p n", p=P)
    w1_cols = w1.rearrange("(h t p) (g c) -> h g p t c", p=P, h=2, c=P)
    w0_cols = w0.rearrange("(t p) (k c) -> k p t c", p=P, c=P)
    mask_rows = mask.rearrange("b (k p) n -> b k p n", p=P)
    x_rows = x.rearrange("b (t p) n -> b p t n", p=P)
    out_rows = out.rearrange("b (t p) (h n) -> b t h p n", p=P, h=2)
    a2_rows = a2.rearrange("s (t p) r -> s p t r", p=P)
    a3_rows = a3.rearrange("s (t p) r -> s p t r", p=P)

    w0t_dram = nc.dram_tensor("w0t_dram", [KT, P, D], F32, kind="Internal").ap()
    g_dram = nc.dram_tensor("g_dram", [NB, 2, 2, R, D], F32, kind="Internal").ap()
    y_dram = nc.dram_tensor("y_dram", [NB, R], F32, kind="Internal").ap()

    base = (nc.sbuf_base + 31) // 32 * 32
    names = {}

    def at(name, shape, dt, offset):
        return nc.alloc_sbuf_tensor_at(name, shape, dt, offset=offset)

    KB = 1024
    reg_p = base
    reg_ce = reg_p + 64 * KB
    reg_z1 = reg_ce + 16 * KB
    reg_ring = reg_z1 + 80 * KB
    reg_z3 = reg_ring + 16 * KB
    reg_la = reg_z3 + 21 * KB
    reg_b2 = reg_la + 4 * KB
    reg_c = reg_b2 + 4 * KB

    Ph = at("P_hi", [P, KT, D], F32R, reg_p)
    Pl = at("P_lo", [P, KT, D], F32R, reg_p + 32 * KB)
    Ceh = at("C_hi", [P, KT, 2, NB, R], F32R, reg_ce)
    Cel = at("C_lo", [P, KT, 2, NB, R], F32R, reg_ce + 8 * KB)
    w2n = at("w2_nat", [P, KT, D], F32, reg_p)
    lo = reg_p + 32 * KB
    b3n = at("b3_nat", [P, D], F32, lo)
    b3t = at("b3_t", [P, KT, NBR], F32, lo + 4 * KB)
    b2n = at("b2_nat", [P, D], F32, lo + 8 * KB)
    b2t = at("b2_t", [P, KT, NBR], F32, lo + 12 * KB)
    a3n = at("a3_nat", [P, KT, NB, R], F32, lo + 16 * KB)
    a3t = at("a3_t", [P, D], F32, lo + 20 * KB)
    a2n = at("a2_nat", [P, KT, NB, R], F32, lo + 24 * KB)
    lbn = at("lb_nat", [P, KT, RL], F32, lo + 28 * KB)
    own = at("own_batch", [P, NB, R], F32, lo + 30 * KB)
    b3b2 = at("b3_b2_t", [P, NBR], F32, lo + 30 * KB + 512)
    Wh = at("w2_hi", [P, KT, EXT], F32R, reg_z1)
    Wl = at("w2_lo", [P, KT, EXT], F32R, reg_z1 + 40 * KB)
    w0t = at("w0_t", [P, KT, D], F32, reg_z1)
    Mh = at("m_hi", [P, MR, HALF], F32R, reg_z1 + 32 * KB)
    Ml = at("m_lo", [P, MR, HALF], F32R, reg_z1 + 40 * KB)
    xTh = at("x_t_hi", [P, KT, T], F32R, reg_z1 + 48 * KB)
    xTl = at("x_t_lo", [P, KT, T], F32R, reg_z1 + 56 * KB)
    x1h = at("x1_t_hi", [P, KT, T], F32R, reg_z1 + 64 * KB)
    x1l = at("x1_t_lo", [P, KT, T], F32R, reg_z1 + 72 * KB)
    ring_i = at("mask_ring", [P, MR, D], I32, reg_ring)
    ring_f = at("merged_ring", [P, MR, D], F32, reg_ring)
    gah = at("ga_hi", [P, D], F32R, reg_ring)
    gal = at("ga_lo", [P, D], F32R, reg_ring + 4 * KB)
    a3h = at("a3_hi", [P, D], F32R, reg_ring + 8 * KB)
    a3l = at("a3_lo", [P, D], F32R, reg_ring + 12 * KB)
    pooled = at("pooled", [P, 2, HALF], F32, reg_ring)
    term_b = at("term_b", [P, HALF], F32, reg_ring + 4 * KB)
    term_c = at("term_c", [P, HALF], F32, reg_ring + 6 * KB)
    w0_out = at("w0_out", [P, D], F32, reg_ring + 8 * KB)
    w0n = at("w0_nat", [P, KT, P], F32, reg_ring + 12 * KB)
    raw = at("w1_raw", [P, 2, HT, P], F32, reg_z3)
    wn = at("w1_norm", [P, HT, P], F32, reg_z3 + 4 * KB)
    term_a = at("term_a", [P, HALF], F32, reg_z3 + 6 * KB)
    W1h = at("w1_hi", [P, KT, P], F32R, reg_z3 + 8 * KB)
    W1l = at("w1_lo", [P, KT, P], F32R, reg_z3 + 12 * KB)
    acc = at("acc", [P, 2, HALF], F32, reg_z3 + 16 * KB)
    xn = at("x_nat", [P, TT, D], F32, reg_z3)
    Cb = at("c_batch", [P, KT, 4, 2, R], F32R, reg_z3 + 8 * KB)
    Gs = at("g_batch", [P, D], F32R, reg_z3 + 12 * KB)
    staged = at("out_staged", [P, 2, HALF], F32, reg_z3 + 16 * KB)
    Us = at("u_batch", [P, T], F32R, reg_z3 + 20 * KB)
    la = at("lora_a", [P, D], F32, reg_la)
    lbt = at("lora_b_t", [P, D], F32, reg_b2)
    b2all = at("b2_rows", [P, D], F32, reg_b2)

    off = [reg_c]

    def const(name, shape):
        n = 4
        for s in shape[1:]:
            n *= s
        t = at(name, shape, F32, off[0])
        off[0] += (n + 31) // 32 * 32
        return t

    ident = const("ident", [P, P])
    cb = const("codebook_rows", [P, NCB])
    cbn = const("codebook_neg", [P, NCB])
    mx = const("codebook_max", [P, 1])
    rmx = const("codebook_rmax", [P, 1])
    th = const("thresholds", [P, NTH])
    dd = const("steps", [P, NTH])
    cf = const("coeff_rows", [P, NB])
    now_tab = const("batch_cols", [P, NB, 3])
    now = const("batch_now", [P, 3])
    sc_now = const("scale_now", [P, KT])
    b0c = const("b0_cols", [P, KT])
    b2c = const("b2_cols", [P, KT])
    sc = const("scale", [P, KT, G])
    rs = const("scale_recip", [P, KT, G])
    yc = const("y_col", [P, 1])

    with ExitStack() as ctx:
        def sem(name):
            return ctx.enter_context(nc.semaphore(name))

        bank = [ctx.enter_context(nc.psum_tensor(f"bank{i}", [P, 512], F32)) for i in range(3)]
        dps = [ctx.enter_context(nc.psum_tensor(f"delta{i}", [P, D], F32)) for i in range(2)]
        bank += [dps[0][:, 0:512], dps[0][:, 512:1024], dps[1][:, 0:512], dps[1][:, 512:1024]]
        bank += [ctx.enter_context(nc.psum_tensor("bank7", [P, 512], F32))]

        s = {n: sem(n) for n in """small_in late_in lora_small w1_in0 w1_in1 a2_in b2_in a3_in b3_in w0_in w0_out_stored g_stored y_stored
            ub_in b2row_in x_in g_in ident_set ident_zero own_a own_b own_set ub_zero
            prep_done prep_hi prep_lo w2_eye ab_hi ab_lo b3b2_set y_set gsum_set scale_set cb_set coef_set ga_hi ga_lo
            delta_done raw_used eye_done delta_used terms pool_added scaled acc_ready eff_set w1_hi_set w1_ready
            p_used p_done p_hi p_ready w0_eye w0_tr w0_evac dve_step pool_step act_step
            s_set v_set h_set m_ready m_used l0_done x1_hi x1_ready t_done xt_hi xt_ready u_done u_hi u_ready c_ready
            out_done out_added out_st0 out_st1 lora_pad now_set scale_now""".split()}
        w2_in = [sem(f"w2_in{t}") for t in range(KT)]
        w0t_in = [sem(f"w0t_in{t}") for t in range(KT)]
        mask_in = [sem(f"mask_in{t}") for t in range(MR)]
        w1_in = [s["w1_in0"], s["w1_in1"]]
        out_stored = [s["out_st0"], s["out_st1"]]
        block = ctx.enter_context(nc.Block())

        STAGES = [("lbt", 0), ("lbt", 1), ("b3t", 2), ("b3t", 3), ("a3t", 4), ("a3t", 5), ("b2t", 6), ("b2t", 7),
                  ("b3b2", 0)]
        W2T0 = len(STAGES)
        W2BANK = [4, 5, 6, 7]
        GA0 = W2T0 + 2 * KT
        V0 = GA0 + 2
        HI_V = 8 + 2 * KT

        @block.sync
        def _(sp):
            def row(v):
                return v.rearrange("(o n) -> o n", o=1)

            def raw_load(g, h):
                sp.dma_start(raw[:, h], w1_cols[h, g]).then_inc(w1_in[h], 16)

            sp.dma_start(lbn[:, :, :], lora_b.rearrange("(t p) r -> p t r", p=P)).then_inc(s["lora_small"], 16)
            sp.dma_start(sc[:, :, :], scale_log.rearrange("(t p) g o -> p t (g o)", p=P)).then_inc(s["small_in"], 16)
            sp.dma_start(cb[:, :], row(codebook).broadcast_to([P, NCB])).then_inc(s["small_in"], 16)
            sp.dma_start(la[0:RL, :], lora_a).then_inc(s["lora_small"], 16)
            for h in range(2):
                raw_load(0, h)
            for t in range(KT):
                sp.dma_start(w2n[:, t], w2_rows[t]).then_inc(w2_in[t], 16)
            with sp.Fori(0, NB) as b:
                slot = sp.value_load(row(tok2)[0:1, bass.ds(b, 1)], min_val=0, max_val=a2.shape[0] - 1)
                sp.dma_start(a2n[:, :, bass.ds(b, 1), :], a2_rows[bass.ds(slot, 1)].rearrange("s p t r -> p t s r")).then_inc(s["a2_in"], 16)
            sp.dma_start(cf[:, :], row(coeff).broadcast_to([P, NB])).then_inc(s["late_in"], 16)
            sp.dma_start(b0c[:, :], b0.rearrange("(t p) -> p t", p=P), allow_slow_non_contiguous=True).then_inc(s["late_in"], 16)
            sp.wait_ge(s["y_set"], 1)
            sp.dma_start(y_dram.rearrange("b (r o) -> (b r) o", o=1), yc[:, :]).then_inc(s["y_stored"], 16)
            sp.wait_ge(s["y_stored"], 16)
            sp.wait_ge(s["ub_zero"], 1)
            for q in range(3):
                sp.dma_start(now_tab[q * 32 + R:q * 32 + 2 * R, :, 2], y_dram.rearrange("b r -> r b"), allow_slow_non_contiguous=True).then_inc(s["ub_in"], 16)
            sp.wait_ge(s["ga_hi"], 2)
            sp.wait_ge(s["ga_lo"], 2)
            for part, (ga, a3p) in enumerate(((gah, a3h), (gal, a3l))):
                sp.dma_start(g_dram[:, part, 0], ga[:, :].bitcast(F32)).then_inc(s["g_stored"], 16)
                sp.dma_start(g_dram[:, part, 1], a3p[:, :].bitcast(F32)).then_inc(s["g_stored"], 16)
            sp.wait_ge(s["g_stored"], 64)
            sp.dma_start(w0n[:, :, :], w0_cols[0]).then_inc(s["w0_in"], 16)
            for h in range(2):
                sp.wait_ge(s["raw_used"], 1 + h)
                raw_load(1, h)

            def group(g, load_w1, load_w0):
                if load_w1:
                    for h in range(2):
                        sp.wait_ge(s["raw_used"], 2 * (g + 1) + h + 1)
                        sp.dma_start(raw[:, h], w1_cols[h, bass.ds(g + 2, 1)].rearrange("g p t c -> (g p) t c")).then_inc(w1_in[h], 16)
                if load_w0:
                    sp.wait_ge(s["w0_tr"], 2 * (g + 1))
                    sp.dma_start(w0n[:, :, :], w0_cols[bass.ds(g + 1, 1)].rearrange("k p t c -> (k p) t c")).then_inc(s["w0_in"], 16)
                sp.wait_ge(s["w0_evac"], 2 * (g + 1))
                sp.dma_start(w0t_dram[bass.ds(g, 1)].rearrange("k p n -> (k p) n"), w0_out[:, :]).then_inc(s["w0_out_stored"], 16)

            with sp.Fori(0, (G - 2) // 2) as j:
                group(2 * j, True, True)
                group(2 * j + 1, True, True)
            group(G - 2, False, True)
            group(G - 1, False, False)
            sp.wait_ge(s["delta_done"], 2 * G)
            sp.dma_start(b2all[:, :], row(b2).broadcast_to([P, D])).then_inc(s["b2row_in"], 16)

            def load_x(b):
                sp.dma_start(xn[:, :, :], x_rows[b] if isinstance(b, int) else x_rows[bass.ds(b, 1)].rearrange("b p t n -> (b p) t n")).then_inc(s["x_in"], 16)

            def load_mask(b, k):
                src = mask_rows[b, k] if isinstance(b, int) else mask_rows[bass.ds(b, 1), k].rearrange("b p n -> (b p) n")
                sp.dma_start(ring_i[:, k % MR], src).then_inc(mask_in[k % MR], 16)

            sp.wait_ge(s["eff_set"], 2 * G)
            load_x(0)
            load_mask(0, 0)
            load_mask(0, 1)
            sp.wait_ge(s["w0_out_stored"], 16 * G)
            load_mask(0, 2)
            load_mask(0, 3)
            for k in range(KT):
                sp.wait_ge(s["p_used"], KT * (G - 1) + k + 1)
                sp.dma_start(w0t[:, k], w0t_dram[k]).then_inc(w0t_in[k], 16)

            def store(b, t):
                for h in range(2):
                    sp.wait_ge(s["out_added"], 4 * b + 2 * t + h + 1)
                    dst = out_rows[b, t, h] if isinstance(b, int) else out_rows[bass.ds(b, 1), t, h].rearrange("b p n -> (b p) n")
                    sp.dma_start(dst, staged[:, h]).then_inc(out_stored[h], 16)

            def batch(b, first=False, last=False):
                for k in range(MR, KT):
                    if k == MR + 2 and not first:
                        store(b - 1, 1)
                    sp.wait_ge(s["m_ready"], 2 * KT * b + 2 * (k - MR) + 2)
                    load_mask(b, k)
                if first:
                    sp.wait_ge(s["p_used"], KT * G)
                else:
                    sp.wait_ge(s["out_done"], 4 * b)
                for part, rows in ((0, 0), (0, 32), (1, 64), (0, 96)):
                    src = g_dram[b, part] if isinstance(b, int) else g_dram[bass.ds(b, 1), part].rearrange("b s r n -> (b s) r n")
                    sp.dma_start(Gs[rows:rows + 32, :].bitcast(F32), src).then_inc(s["g_in"], 16)
                if not last:
                    sp.wait_ge(s["t_done"], 4 * (b + 1))
                    load_x(b + 1)
                    for k in range(MR):
                        sp.wait_ge(s["m_ready"], 2 * KT * b + 2 * (k + MR) + 2)
                        load_mask(b + 1, k)
                store(b, 0)

            batch(0, first=True)
            with sp.Fori(1, NB - 1) as b:
                batch(b)
            batch(NB - 1, last=True)
            store(NB - 1, 1)
            for h in range(2):
                sp.wait_ge(out_stored[h], 16 * 2 * NB)

        @block.gpsimd
        def _(pool):
            nc.gpsimd.memset(ident[:, :], 0.0).then_inc(s["ident_zero"], 1)
            nc.gpsimd.memset(own[:, :, :], 1.0).then_inc(s["own_a"], 1)
            pool.wait_ge(s["ident_zero"], 1)
            nc.gpsimd.affine_select(out=ident[:, :], in_=ident[:, :], compare_op=ALU.not_equal, fill=1.0, base=0,
                                    pattern=[[-1, P]], channel_multiplier=1).then_inc(s["ident_set"], 1)
            pool.wait_ge(s["own_a"], 1)
            nc.gpsimd.affine_select(out=own[:, :, :], in_=own[:, :, :], compare_op=ALU.is_ge, fill=0.0, base=0,
                                    pattern=[[-R, NB], [0, R]], channel_multiplier=1).then_inc(s["own_b"], 1)
            pool.wait_ge(s["own_b"], 1)
            nc.gpsimd.affine_select(out=own[:, :, :], in_=own[:, :, :], compare_op=ALU.is_ge, fill=0.0, base=R - 1,
                                    pattern=[[R, NB], [0, R]], channel_multiplier=-1).then_inc(s["own_set"], 1)
            step = Order(pool, s["pool_step"])

            def sums(q, h):
                n = 2 * q + h
                pl = pooled[:, h]
                pool.wait_ge(s["terms"], 4 * n + 1)
                step.did(nc.gpsimd.tensor_tensor(pl, pl, term_b[:, :], ALU.add))
                pool.wait_ge(s["terms"], 4 * n + 2)
                step.wait()
                step.did(nc.gpsimd.tensor_tensor(pl, pl, term_c[:, :], ALU.add))
                pool.wait_ge(s["terms"], 4 * n + 3)
                step.wait()
                step.did(nc.gpsimd.tensor_tensor(pl, pl, term_b[:, :], ALU.add))
                pool.wait_ge(s["terms"], 4 * n + 4)
                step.wait()
                nc.gpsimd.tensor_tensor(pl, pl, acc[:, h], ALU.add).then_inc(s["pool_added"], 1)

            def group(g, quant):
                pool.wait_ge(s["w0_in"], 16 * (g + 1))
                blk = w0n[:, bass.ds(g, 1), :].rearrange("p k c -> p (k c)")
                nc.gpsimd.tensor_tensor(blk, blk, ident[:, :], ALU.add).then_inc(s["w0_eye"], 1)
                if quant:
                    for h in range(2):
                        sums(g + 1, h)

            for h in range(2):
                sums(0, h)
            per = 2 * 6
            pairs = (G - 2) // 2
            start = step.n
            with pool.Fori(0, pairs) as j:
                step.rebase(start + j * per * 1)
                group(2 * j, True)
                group(2 * j + 1, True)
                assert step.n == per
            step.rebase(start + pairs * per)
            group(G - 2, True)
            group(G - 1, False)

            def batch(b, first=False):
                if first:
                    pool.wait_ge(s["p_ready"], 3 * G)
                    pool.wait_ge(s["p_hi"], 3 * G)
                else:
                    pool.wait_ge(s["u_done"], b)
                for j in range(4):
                    src = (Ceh if j < 3 else Cel)[:, :, :, bass.ds(b, 1), :].rearrange("p k s b r -> p k s (b r)").bitcast(F32)
                    ins = nc.gpsimd.tensor_copy(Cb[:, :, j], src)
                    ins.then_inc(s["c_ready"], 1)

            batch(0, first=True)
            with pool.Fori(1, NB) as b:
                batch(b)

        @block.scalar
        def _(act):
            def token(tok, b, n):
                return act.value_load(tok.rearrange("(o n) -> o n", o=1)[0:1, b:b + 1], min_val=0, max_val=n - 1)

            for b in range(NB):
                slot = token(tok3, b, a3.shape[0])
                act.dma_start(b3n[b * R:(b + 1) * R, :], bb3[bass.ds(slot, 1)].rearrange("s r n -> (s r) n")).then_inc(s["b3_in"], 16)
                act.dma_start(a3n[:, :, b, :], a3_rows[bass.ds(slot, 1)].rearrange("s p t r -> (s p) t r")).then_inc(s["a3_in"], 16)
            for b in range(NB):
                slot = token(tok2, b, a2.shape[0])
                act.dma_start(b2n[b * R:(b + 1) * R, :], bb2[bass.ds(slot, 1)].rearrange("s r n -> (s r) n")).then_inc(s["b2_in"], 16)
            act.dma_start(b2c[:, :], b2.rearrange("(t p) -> p t", p=P), allow_slow_non_contiguous=True).then_inc(s["b2_in"], 16)
            act.wait_ge(s["small_in"], 32)
            nc.scalar.activation(sc[:, :, :], sc[:, :, :], ACT.Exp).then_inc(s["scale_set"], 1)
            act.wait_ge(s["scale_set"], 1)

            for n, dst in enumerate((lbt, b3t, a3t, b2t)):
                for h in range(2):
                    act.wait_ge(s["prep_done"], 2 * n + h + 1)
                    src = bank[STAGES[2 * n + h][1]]
                    if n == 0:
                        nc.scalar.mul(dst[0:RL, h * 512:(h + 1) * 512], src[0:RL, :], L1_SCALE).then_inc(s["prep_hi"], 1)
                    elif n == 2:
                        nc.scalar.copy(dst[:, h * 512:(h + 1) * 512], src[:, :]).then_inc(s["prep_hi"], 1)
                    else:
                        nc.scalar.copy(dst[:, h * HT:(h + 1) * HT, :], src[:, :]).then_inc(s["prep_hi"], 1)
            for t in range(KT):
                for h in range(2):
                    i = 2 * t + h
                    act.wait_ge(s["prep_done"], W2T0 + i + 1)
                    nc.scalar.copy(Wh[:, h * HT:(h + 1) * HT, t * P:(t + 1) * P], bank[W2BANK[i % 4]][:, :]).then_inc(s["prep_hi"], 1)
            act.wait_ge(s["a2_in"], 16 * NB)
            nc.scalar.copy(Wh[:, :, D:D + NBR], a2n[:, :, :, :]).then_inc(s["ab_hi"], 1)
            act.wait_ge(s["gsum_set"], 2)
            nc.scalar.mul(gah[:, :], b2n[:, :], L2_SCALE).then_inc(s["ga_hi"], 1)
            act.wait_ge(s["prep_hi"], 6)
            nc.scalar.copy(a3h[:, :], a3t[:, :]).then_inc(s["ga_hi"], 1)
            for h in range(2):
                act.wait_ge(s["prep_done"], V0 + h + 1)
                nc.scalar.copy(Wh[:, h * HT:(h + 1) * HT, D + NBR:EXT], bank[h][:, :]).then_inc(s["prep_hi"], 1)

            def scaled(q, h, first=False):
                if h == 0:
                    if not first:
                        act.wait_ge(s["scaled"], KT * q)
                        act.wait_ge(s["scale_set"], 1)
                    nc.scalar.copy(sc_now[:, :], sc[:, :, bass.ds(q, 1)].rearrange("p t g -> p (t g)")).then_inc(s["scale_now"], 1)
                    act.wait_ge(s["scale_now"], q + 1)
                act.wait_ge(s["pool_added"], 2 * q + h + 1)
                for t in range(HT):
                    blk = pooled[:, h, t * P:(t + 1) * P]
                    nc.scalar.activation(blk, blk, ACT.Copy, scale=sc_now[:, h * HT + t:h * HT + t + 1]).then_inc(s["scaled"], 1)

            def w1_hi(q, h, first=False):
                act.wait_ge(s["eff_set"], 2 * q + h + 1)
                if not first:
                    act.wait_ge(s["p_used"], KT * (q - 1) + (h + 1) * HT)
                nc.scalar.copy(W1h[:, h * HT:(h + 1) * HT, :], acc[:, h]).then_inc(s["w1_hi_set"], 1)

            def p_hi(g):
                for n in range(3):
                    if n < 2:
                        act.wait_ge(s["p_done"], 2 * g + n + 1)
                        dst = Ph[:, bass.ds(g, 1), n * 512:(n + 1) * 512].rearrange("p k n -> p (k n)")
                        nc.scalar.copy(dst, bank[n][:, :]).then_inc(s["p_hi"], 1)
                    else:
                        act.wait_ge(s["p_used"], KT * (g + 1))
                        dst = Ceh[:, bass.ds(g, 1)].rearrange("p k s b r -> p (k s b r)")
                        nc.scalar.copy(dst, bank[n][:, 0:2 * NBR]).then_inc(s["p_hi"], 1)

            def w0_evac(g, first=False):
                for h in range(2):
                    act.wait_ge(s["w0_tr"], 2 * g + h + 1)
                    if not first:
                        act.wait_ge(s["w0_out_stored"], 16 * g)
                    nc.scalar.copy(w0_out[:, h * 512:(h + 1) * 512], bank[7][:, :]).then_inc(s["w0_evac"], 1)

            for h in range(2):
                scaled(0, h, first=True)
                w1_hi(0, h, first=True)

            def group(g, quant, first=False):
                w0_evac(g, first)
                if quant:
                    scaled(g + 1, 0)
                    scaled(g + 1, 1)
                    w1_hi(g + 1, 0)
                p_hi(g)
                if quant:
                    w1_hi(g + 1, 1)

            group(0, True, first=True)
            group(1, True)
            with act.Fori(1, (G - 2) // 2) as j:
                group(2 * j, True)
                group(2 * j + 1, True)
            group(G - 2, True)
            group(G - 1, False)

            act.wait_ge(s["late_in"], 32)

            def signs(b, k):
                act.wait_ge(mask_in[k % MR], 16 * (2 * b + k // MR + 1))
                nc.scalar.activation(ring_f[:, k % MR], ring_i[:, k % MR], ACT.Identity,
                                     bias=now[:, 1:2], scale=now[:, 0:1]).then_inc(s["s_set"], 1)

            def m_hi(b, k, first):
                act.wait_ge(s["v_set"], KT * b + k + 1)
                for h in range(2):
                    n = 2 * k + h
                    if not (first and n < MR):
                        act.wait_ge(s["m_used"], 2 * KT * b + n - MR + 1)
                    nc.scalar.copy(Mh[:, n % MR], ring_f[:, k % MR, h * HALF:(h + 1) * HALF]).then_inc(s["h_set"], 1)

            def x_hi(b):
                for i in range(4):
                    act.wait_ge(s["t_done"], 4 * b + i + 1)
                    nc.scalar.copy(xTh[:, 2 * i:2 * i + 2, :], bank[6 + i % 2][:, :]).then_inc(s["xt_hi"], 1)

            def batch(b, first=False, last=False):
                if not first:
                    act.wait_ge(s["u_ready"], b)
                nc.scalar.copy(now[:, :], now_tab[:, bass.ds(b, 1), :].rearrange("p b c -> p (b c)")).then_inc(s["now_set"], 1)
                act.wait_ge(s["now_set"], b + 1)
                for k in range(2):
                    signs(b, k)
                for k in range(2):
                    m_hi(b, k, first)
                for k in range(2, MR + 2):
                    signs(b, k)
                for k in range(2, KT):
                    m_hi(b, k, first)
                    if 0 <= k - MR < KT - MR - 2:
                        signs(b, k + 2)
                for o in range(KT):
                    if o % HT == 0:
                        act.wait_ge(s["l0_done"], 2 * b + o // HT + 1)
                    elif o % 2 == 0:
                        act.wait_ge(s["m_used"], 2 * KT * (b + 1) - 1 + o // HT)
                    nc.scalar.activation(x1h[:, o], bank[o // 2 if o // 2 < 4 else 0][:, (o % 2) * T:(o % 2 + 1) * T], ACT.Identity,
                                         bias=b0c[:, o:o + 1]).then_inc(s["x1_hi"], 1)
                if not last:
                    x_hi(b + 1)
                act.wait_ge(s["u_done"], b + 1)
                nc.scalar.activation(Us[:, :], bank[6][:, 0:T], ACT.Identity, bias=now[:, 2:3]).then_inc(s["u_hi"], 1)

            x_hi(0)
            act.wait_ge(s["coef_set"], 2)
            act.wait_ge(s["ub_in"], 48)
            batch(0, first=True)
            with act.Fori(1, NB - 1) as b:
                batch(b)
            batch(NB - 1, last=True)

        @block.vector
        def _(dve):
            step = Order(dve, s["dve_step"])

            def link(ins):
                step.did(ins)
                step.wait()

            nc.vector.memset(now_tab[:, :, :], 0.0).then_inc(s["ub_zero"], 1)
            nc.vector.memset(la[RL:P, :], 0.0).then_inc(s["lora_pad"], 1)
            nc.vector.memset(lbt[RL:P, :], 0.0).then_inc(s["lora_pad"], 1)
            dve.wait_ge(s["small_in"], 32)
            link(nc.vector.tensor_scalar(cbn[:, :], cb[:, :], -1.0, None, ALU.mult))
            link(nc.vector.tensor_tensor(cbn[:, :], cbn[:, :], cb[:, :], ALU.max))
            link(nc.vector.reduce_max(mx[:, :], cbn[:, :], AXX))
            link(nc.vector.tensor_scalar(mx[:, :], mx[:, :], 1e-8, None, ALU.max))
            link(nc.vector.reciprocal(rmx[:, :], mx[:, :]))
            link(nc.vector.tensor_scalar(cb[:, :], cb[:, :], rmx[:, 0:1], None, ALU.mult))
            link(nc.vector.tensor_tensor(dd[:, :], cb[:, 1:NCB], cb[:, 0:NTH], ALU.subtract))
            link(nc.vector.tensor_tensor(th[:, :], cb[:, 1:NCB], cb[:, 0:NTH], ALU.add))
            link(nc.vector.tensor_scalar(th[:, :], th[:, :], 0.5, None, ALU.mult))

            def c(i):
                return th[:, i:i + 1]

            link(nc.vector.tensor_tensor(c(1), c(1), c(3), ALU.min))
            link(nc.vector.tensor_tensor(c(5), c(5), c(3), ALU.max))
            link(nc.vector.tensor_tensor(c(0), c(0), c(1), ALU.min))
            link(nc.vector.tensor_tensor(c(2), c(2), c(1), ALU.max))
            link(nc.vector.tensor_tensor(c(2), c(2), c(3), ALU.min))
            link(nc.vector.tensor_tensor(c(4), c(4), c(3), ALU.max))
            link(nc.vector.tensor_tensor(c(4), c(4), c(5), ALU.min))
            link(nc.vector.tensor_tensor(c(6), c(6), c(5), ALU.max))
            dve.wait_ge(s["scale_set"], 1)
            link(nc.vector.reciprocal(rs[:, :, :], sc[:, :, :]))
            dve.wait_ge(s["ident_set"], 1)
            for t in range(KT):
                dve.wait_ge(w2_in[t], 16)
                blk = w2n[:, t, t * P:(t + 1) * P]
                nc.vector.tensor_tensor(blk, blk, ident[:, :], ALU.add).then_inc(s["w2_eye"], 1)
                if t == 0:
                    dve.wait_ge(s["prep_done"], W2T0)
                    dve.wait_ge(s["own_set"], 1)
                    nc.vector.tensor_tensor(b3b2[:, :], bank[0][:, 0:NBR], own[:, :, :].rearrange("p b r -> p (b r)"), ALU.mult).then_inc(s["b3b2_set"], 1)
                    nc.vector.tensor_copy(yc[:, :], bank[0][:, NBR:NBR + 1]).then_inc(s["y_set"], 1)
                if t >= 1:
                    for h in range(2):
                        i = 2 * (t - 1) + h
                        dve.wait_ge(s["prep_hi"], 8 + i + 1)
                        dst = slice(h * HT, (h + 1) * HT), slice((t - 1) * P, t * P)
                        nc.vector.tensor_tensor(Wl[:, dst[0], dst[1]], bank[W2BANK[i % 4]][:, :], Wh[:, dst[0], dst[1]].bitcast(F32),
                                                ALU.subtract).then_inc(s["prep_lo"], 1)
            for h in range(2):
                i = 2 * (KT - 1) + h
                dve.wait_ge(s["prep_hi"], 8 + i + 1)
                dst = slice(h * HT, (h + 1) * HT), slice((KT - 1) * P, D)
                nc.vector.tensor_tensor(Wl[:, dst[0], dst[1]], bank[W2BANK[i % 4]][:, :], Wh[:, dst[0], dst[1]].bitcast(F32),
                                        ALU.subtract).then_inc(s["prep_lo"], 1)
            for h in range(2):
                dve.wait_ge(s["prep_done"], GA0 + h + 1)
                cols = slice(h * 512, (h + 1) * 512)
                nc.vector.tensor_tensor(b2n[:, cols], b2n[:, cols], bank[2 + h][:, :], ALU.add).then_inc(s["gsum_set"], 1)
            dve.wait_ge(s["ab_hi"], 1)
            nc.vector.tensor_tensor(Wl[:, :, D:D + NBR], a2n[:, :, :, :].rearrange("p t b r -> p t (b r)"), Wh[:, :, D:D + NBR].bitcast(F32), ALU.subtract).then_inc(s["ab_lo"], 1)
            dve.wait_ge(s["ga_hi"], 1)
            nc.vector.scalar_tensor_tensor(out=gal[:, :], in0=b2n[:, :], scalar=L2_SCALE, in1=gah[:, :].bitcast(F32),
                                           op0=ALU.mult, op1=ALU.subtract).then_inc(s["ga_lo"], 1)
            dve.wait_ge(s["ga_hi"], 2)
            nc.vector.tensor_tensor(a3l[:, :], a3t[:, :], a3h[:, :].bitcast(F32), ALU.subtract).then_inc(s["ga_lo"], 1)
            for h in range(2):
                dve.wait_ge(s["prep_hi"], HI_V + h + 1)
                dst = Wl[:, h * HT:(h + 1) * HT, D + NBR:EXT]
                nc.vector.tensor_tensor(dst, bank[h][:, :], Wh[:, h * HT:(h + 1) * HT, D + NBR:EXT].bitcast(F32), ALU.subtract).then_inc(s["prep_lo"], 1)

            def per_group(tile, q, h):
                return tile[:, h * HT:(h + 1) * HT, bass.ds(q, 1)].broadcast_to([P, HT, P])

            def terms(q, h, par, first=False, reused=True):
                n = 2 * q + h
                if not first:
                    dve.wait_ge(s["terms"], 4 * n)
                dve.wait_ge(w1_in[h], 16 * (q + 1))
                dve.wait_ge(s["delta_done"], n + 1)
                ins = nc.vector.tensor_tensor(wn[:, :, :], raw[:, h], dps[par][:, h * 512:(h + 1) * 512], ALU.add)
                ins.then_inc(s["raw_used"], 1)
                dve.wait_ge(s["raw_used"], n + 1)
                link(nc.vector.tensor_tensor(wn[:, :, :], wn[:, :, :], per_group(rs, q, h), ALU.mult))
                flat = wn[:, :, :].rearrange("p t c -> p (t c)")

                def term(i, dst):
                    return nc.vector.tensor_scalar(dst, flat, th[:, i:i + 1], dd[:, i:i + 1], ALU.is_gt, ALU.mult)

                if not first:
                    dve.wait_ge(s["pool_added"], n)
                if reused:
                    dve.wait_ge(s["w1_ready"], n - 1)
                link(term(3, pooled[:, h]))
                term(4, term_b[:, :]).then_inc(s["terms"], 1)
                term(5, term_c[:, :]).then_inc(s["terms"], 1)
                step.did(term(0, acc[:, h]))
                link(term(1, term_a[:, :]))
                link(nc.vector.scalar_tensor_tensor(out=acc[:, h], in0=acc[:, h], scalar=cb[:, 0:1], in1=term_a[:, :],
                                                    op0=ALU.add, op1=ALU.add))
                link(term(2, term_a[:, :]))
                dve.wait_ge(s["pool_step"], 3 * n + 1)
                term(6, term_b[:, :]).then_inc(s["terms"], 1)
                nc.vector.tensor_tensor(acc[:, h], acc[:, h], term_a[:, :], ALU.add).then_inc(s["terms"], 1)

            def effective(q, h, par):
                dve.wait_ge(s["scaled"], HT * (2 * q + h + 1))
                dve.wait_ge(s["eye_done"], q + 1)
                nc.vector.tensor_tensor(acc[:, h], pooled[:, h], dps[par][:, h * 512:(h + 1) * 512], ALU.add).then_inc(s["eff_set"], 1)

            def w1_lo(q, h):
                dve.wait_ge(s["w1_hi_set"], 2 * q + h + 1)
                nc.vector.tensor_tensor(W1l[:, h * HT:(h + 1) * HT, :], acc[:, h], W1h[:, h * HT:(h + 1) * HT, :].bitcast(F32),
                                        ALU.subtract).then_inc(s["w1_ready"], 1)

            def p_lo(g):
                for n in range(3):
                    dve.wait_ge(s["p_hi"], 3 * g + n + 1)
                    if n < 2:
                        cols = slice(n * 512, (n + 1) * 512)
                        hi = Ph[:, bass.ds(g, 1), cols].rearrange("p k n -> p (k n)").bitcast(F32)
                        lo_ = Pl[:, bass.ds(g, 1), cols].rearrange("p k n -> p (k n)")
                        nc.vector.tensor_tensor(lo_, bank[n][:, :], hi, ALU.subtract).then_inc(s["p_ready"], 1)
                    else:
                        hi = Ceh[:, bass.ds(g, 1)].rearrange("p k s b r -> p (k s b r)").bitcast(F32)
                        lo_ = Cel[:, bass.ds(g, 1)].rearrange("p k s b r -> p (k s b r)")
                        nc.vector.tensor_tensor(lo_, bank[n][:, 0:2 * NBR], hi, ALU.subtract).then_inc(s["p_ready"], 1)

            dve.wait_ge(s["g_stored"], 64)
            for h in range(2):
                terms(0, h, 0, first=(h == 0), reused=False)
            for h in range(2):
                effective(0, h, 0)
                w1_lo(0, h)

            def group(g, par, quant):
                if quant:
                    terms(g + 1, 0, 1 - par)
                    terms(g + 1, 1, 1 - par)
                    effective(g + 1, 0, 1 - par)
                    w1_lo(g + 1, 0)
                    effective(g + 1, 1, 1 - par)
                p_lo(g)
                if quant:
                    w1_lo(g + 1, 1)

            per = 4 * 6
            pairs = (G - 2) // 2
            start = step.n
            with dve.Fori(0, pairs) as j:
                step.rebase(start + j * per)
                group(2 * j, 0, True)
                group(2 * j + 1, 1, True)
                assert step.n == per, step.n
            step.rebase(start + pairs * per)
            group(G - 2, 0, True)
            group(G - 1, 1, False)

            dve.wait_ge(s["late_in"], 32)
            nc.vector.tensor_scalar(now_tab[:, :, 0], cf[:, :], 2.0, None, ALU.mult).then_inc(s["coef_set"], 1)
            nc.vector.tensor_scalar(now_tab[:, :, 1], cf[:, :], -1.0, None, ALU.mult).then_inc(s["coef_set"], 1)

            def merged(b, k, first):
                if first:
                    dve.wait_ge(w0t_in[k], 16)
                dve.wait_ge(s["s_set"], KT * b + k + 1)
                nc.vector.tensor_tensor(ring_f[:, k % MR], ring_f[:, k % MR], w0t[:, k], ALU.add).then_inc(s["v_set"], 1)

            def m_lo(b, k):
                for h in range(2):
                    n = 2 * k + h
                    dve.wait_ge(s["h_set"], 2 * KT * b + n + 1)
                    nc.vector.tensor_tensor(Ml[:, n % MR], ring_f[:, k % MR, h * HALF:(h + 1) * HALF], Mh[:, n % MR].bitcast(F32),
                                            ALU.subtract).then_inc(s["m_ready"], 1)

            def x_lo(b):
                for i in range(4):
                    dve.wait_ge(s["xt_hi"], 4 * b + i + 1)
                    nc.vector.tensor_tensor(xTl[:, 2 * i:2 * i + 2, :], bank[6 + i % 2][:, :], xTh[:, 2 * i:2 * i + 2, :].bitcast(F32),
                                            ALU.subtract).then_inc(s["xt_ready"], 1)

            def out_add(b, t, first=False):
                for h in range(2):
                    dve.wait_ge(s["out_done"], 4 * b + 2 * t + h + 1)
                    if not first:
                        dve.wait_ge(out_stored[h], 16 * (2 * b + t))
                    nc.vector.tensor_tensor(staged[:, h], bank[4 + h][:, :], b2all[:, h * HALF:(h + 1) * HALF], ALU.add).then_inc(s["out_added"], 1)

            def batch(b, first=False, last=False):
                for k in range(2):
                    merged(b, k, first)
                for k in range(2):
                    m_lo(b, k)
                for k in range(2, MR + 2):
                    merged(b, k, first)
                if not first:
                    out_add(b - 1, 1)
                for k in range(2, KT):
                    m_lo(b, k)
                    if 0 <= k - MR < KT - MR - 2:
                        merged(b, k + 2, first)
                for o in range(KT):
                    if o % 2 == 0:
                        dve.wait_ge(s["x1_hi"], KT * b + o + 2)
                    nc.vector.scalar_tensor_tensor(out=x1l[:, o], in0=bank[o // 2][:, (o % 2) * T:(o % 2 + 1) * T], scalar=b0c[:, o:o + 1],
                                                   in1=x1h[:, o].bitcast(F32), op0=ALU.add, op1=ALU.subtract).then_inc(s["x1_ready"], 1)
                if not last:
                    x_lo(b + 1)
                dve.wait_ge(s["u_hi"], b + 1)
                rows = slice(32, 64)
                nc.vector.scalar_tensor_tensor(out=Us[rows, :], in0=bank[6][rows, 0:T], scalar=now[rows, 2:3],
                                               in1=Us[rows, :].bitcast(F32), op0=ALU.add, op1=ALU.subtract).then_inc(s["u_ready"], 1)
                out_add(b, 0, first)

            x_lo(0)
            dve.wait_ge(s["b2row_in"], 16)
            batch(0, first=True)
            with dve.Fori(1, NB - 1) as b:
                batch(b)
            batch(NB - 1, last=True)
            out_add(NB - 1, 1)

        @block.tensor
        def _(pe):
            mm = nc.tensor.matmul

            pe.wait_ge(s["ident_set"], 1)
            pe.wait_ge(s["lora_small"], 32)
            for h in range(2):
                for t in range(HT):
                    ins = nc.tensor.transpose(bank[h][0:RL, t * P:(t + 1) * P], lbn[:, h * HT + t, :], ident[:, :])
                ins.then_inc(s["prep_done"], 1)
            pe.wait_ge(s["b3_in"], 16 * NB)
            for h in range(2):
                for t in range(HT):
                    k = h * HT + t
                    ins = nc.tensor.transpose(bank[2 + h][:, t * P:(t + 1) * P], b3n[:, k * P:(k + 1) * P], ident[:, :])
                ins.then_inc(s["prep_done"], 1)
            pe.wait_ge(s["a3_in"], 16 * NB)
            for h in range(2):
                for t in range(HT):
                    ins = nc.tensor.transpose(bank[4 + h][:, t * P:(t + 1) * P], a3n[:, h * HT + t].rearrange("p b r -> p (b r)"), ident[:, :])
                ins.then_inc(s["prep_done"], 1)
            pe.wait_ge(s["b2_in"], 16 * (NB + 1))
            for h in range(2):
                for t in range(HT):
                    k = h * HT + t
                    ins = nc.tensor.transpose(bank[6 + h][:, t * P:(t + 1) * P], b2n[:, k * P:(k + 1) * P], ident[:, :])
                ins.then_inc(s["prep_done"], 1)
            pe.wait_ge(s["prep_hi"], 8)
            for k in range(KT):
                mm(bank[0][:, 0:NBR], b3t[:, k], b2t[:, k], start=(k == 0), stop=(k == KT - 1), skip_group_check=True)
                ins = mm(bank[0][:, NBR:NBR + 1], b3t[:, k], b2c[:, k:k + 1], start=False, stop=(k == KT - 1), skip_group_check=True)
            ins.then_inc(s["prep_done"], 1)
            for t in range(KT):
                pe.wait_ge(s["w2_eye"], t + 1)
                for h in range(2):
                    i = 2 * t + h
                    if i >= 4:
                        pe.wait_ge(s["prep_lo"], i - 3)
                    for j in range(HT):
                        k = h * HT + j
                        ins = nc.tensor.transpose(bank[W2BANK[i % 4]][:, j * P:(j + 1) * P], w2n[:, t, k * P:(k + 1) * P], ident[:, :])
                    ins.then_inc(s["prep_done"], 1)
            pe.wait_ge(s["b3b2_set"], 1)
            for h in range(2):
                mm(bank[2 + h][:, :], b3b2[:, :], a3t[:, h * 512:(h + 1) * 512], start=True, stop=True).then_inc(s["prep_done"], 1)
            pe.wait_ge(s["y_set"], 1)
            for h in range(2):
                for j in range(HT):
                    k = h * HT + j
                    for t in range(KT):
                        ins = mm(bank[h][:, j * P:(j + 1) * P], w2n[:, t, k * P:(k + 1) * P], b3t[:, t], start=(t == 0), stop=(t == KT - 1))
                ins.then_inc(s["prep_done"], 1)

            def delta(q, par, first=False):
                for h in range(2):
                    pe.wait_ge(s["prep_hi"], 2)
                    if not first:
                        pe.wait_ge(s["eff_set"], 2 * (q - 2) + h + 1)
                    for t in range(HT):
                        k = h * HT + t
                        ins = mm(dps[par][:, k * P:(k + 1) * P], lbt[:, k * P:(k + 1) * P], la[:, bass.ds(q * P, P)],
                                 start=(t == 0), stop=True, skip_group_check=True)
                    ins.then_inc(s["delta_done"], 1)

            def eye(q, par):
                pe.wait_ge(s["raw_used"], 2 * (q + 1))
                mm(dps[par][:, bass.ds(q * P, P)], ident[:, :], ident[:, :], start=False, stop=True, skip_group_check=True).then_inc(s["eye_done"], 1)

            def w0_transpose(g, first=False):
                pe.wait_ge(s["w0_eye"], g + 1)
                for h in range(2):
                    if not (first and h == 0):
                        pe.wait_ge(s["w0_evac"], 2 * g + h)
                    for j in range(HT):
                        ins = nc.tensor.transpose(bank[7][:, j * P:(j + 1) * P], w0n[:, h * HT + j, :], ident[:, :])
                    ins.then_inc(s["w0_tr"], 1)

            pe.wait_ge(s["prep_lo"], 2 * KT)
            pe.wait_ge(s["gsum_set"], 2)
            pe.wait_ge(s["lora_pad"], 2)
            delta(0, 0, first=True)
            eye(0, 0)

            COLS = [(0, 512), (512, 1024), (1024, EXT)]

            def group(g, par, quant, first=False, second=False):
                if quant:
                    if first:
                        delta(g + 1, 1 - par, first=True)
                    else:
                        delta(g + 1, 1 - par)
                w0_transpose(g, first)
                if first:
                    pe.wait_ge(s["ab_lo"], 1)
                    pe.wait_ge(s["prep_lo"], 2 * KT + 2)
                for t in range(KT):
                    if t % HT == 0:
                        pe.wait_ge(s["w1_ready"], 2 * g + t // HT + 1)
                    if quant and t == 6:
                        eye(g + 1, 1 - par)
                    for n, (c0, c1) in enumerate(COLS):
                        if t == 0 and not first:
                            pe.wait_ge(s["p_ready"], 3 * (g - 1) + n + 1)
                        o = bank[n][:, 0:c1 - c0]
                        mm(o, W1h[:, t], Wh[:, t, c0:c1], start=(t == 0), stop=False)
                        mm(o, W1h[:, t], Wl[:, t, c0:c1], start=False, stop=False)
                        ins = mm(o, W1l[:, t], Wh[:, t, c0:c1], start=False, stop=(t == KT - 1))
                        if n == 2:
                            ins.then_inc(s["p_used"], 1)
                        elif t == KT - 1:
                            ins.then_inc(s["p_done"], 1)

            group(0, 0, True, first=True)
            group(1, 1, True)
            with pe.Fori(1, (G - 2) // 2) as j:
                group(2 * j, 0, True)
                group(2 * j + 1, 1, True)
            group(G - 2, 0, True)
            group(G - 1, 1, False)

            def x_transpose(b, i, first=False):
                if i == 0:
                    pe.wait_ge(s["x_in"], 16 * (b + 1))
                if i >= 2:
                    pe.wait_ge(s["xt_ready"], 4 * b + i - 1)
                elif not first:
                    if i == 0:
                        pe.wait_ge(s["u_ready"], b - 1) if not isinstance(b, int) or b >= 2 else None
                    pe.wait_ge(s["xt_ready"], 4 * b)
                elif i == 1:
                    pe.wait_ge(s["w0_evac"], 2 * G)
                for j in range(2):
                    for t in range(TT):
                        k = 2 * i + j
                        c0 = j * T + t * P
                        ins = nc.tensor.transpose(bank[6 + i % 2][:, c0:c0 + P], xn[:, t, k * P:(k + 1) * P], ident[:, :])
                ins.then_inc(s["t_done"], 1)

            def layer0(b, first=False):
                for k in range(KT):
                    for o in range(KT):
                        h = o // HT
                        n = 2 * k + h
                        if o % HT == 0:
                            pe.wait_ge(s["m_ready"], 2 * KT * b + n + 1)
                        if k == 0 and o % 2 == 0 and not first:
                            pe.wait_ge(s["x1_ready"], KT * (b - 1) + o + 2)
                        if k == 0 and o == 0:
                            pe.wait_ge(s["xt_ready"], 4 * (b + 1))
                        dst = bank[o // 2][:, (o % 2) * T:(o % 2 + 1) * T]
                        cols = slice((o % HT) * P, (o % HT + 1) * P)
                        mh, ml = Mh[:, n % MR, cols], Ml[:, n % MR, cols]
                        mm(dst, mh, xTh[:, k], start=(k == 0 and o % 2 == 0), stop=False, skip_group_check=True)
                        mm(dst, mh, xTl[:, k], start=False, stop=False, skip_group_check=True)
                        ins = mm(dst, ml, xTh[:, k], start=False, stop=(k == KT - 1), skip_group_check=True)
                        if o % HT == HT - 1:
                            ins.then_inc(s["m_used"], 1)
                        elif k == KT - 1 and o % 2 == 1:
                            ins.then_inc(s["l0_done"], 1)

            def main(b, t, h, ks, first=False):
                o = bank[4 + h][:, :]
                toks = slice(t * P, (t + 1) * P)
                cols = slice(h * HALF, (h + 1) * HALF)
                for k in ks:
                    if k == 0 and not (first and t == 0):
                        pe.wait_ge(s["out_added"], 4 * b + 2 * t + h - 1)
                    if t == 0 and h == 0:
                        pe.wait_ge(s["x1_ready"], KT * b + k + 1)
                    mm(o, x1h[:, k, toks], Ph[:, k, cols], start=(k == 0), stop=False)
                    mm(o, x1h[:, k, toks], Pl[:, k, cols], start=False, stop=False)
                    mm(o, x1l[:, k, toks], Ph[:, k, cols], start=False, stop=False)

            def rank(b):
                pe.wait_ge(s["c_ready"], 4 * (b + 1))
                for k in range(KT):
                    ck = Cb[:, k].rearrange("p j s r -> p (j s r)")
                    mm(bank[6][:, 0:T], ck, x1h[:, k], start=(k == 0), stop=False)
                    ins = mm(bank[6][:, 0:T], ck, x1l[:, k], start=False, stop=(k == KT - 1))
                ins.then_inc(s["u_done"], 1)

            def close(b, t, h):
                if t == 0 and h == 0:
                    pe.wait_ge(s["u_ready"], b + 1)
                    pe.wait_ge(s["g_in"], 64 * (b + 1))
                mm(bank[4 + h][:, :], Us[:, t * P:(t + 1) * P], Gs[:, h * HALF:(h + 1) * HALF], start=False, stop=True).then_inc(s["out_done"], 1)

            def batch(b, first=False, second=False, last=False):
                layer0(b, first)
                if not last:
                    if first:
                        pe.wait_ge(s["xt_ready"], 4)
                    else:
                        pe.wait_ge(s["u_ready"], b)
                    x_transpose(b + 1, 0, first=True)
                    pe.wait_ge(s["xt_ready"], 4 * (b + 1))
                    x_transpose(b + 1, 1, first=True)
                main(b, 0, 0, range(0, HT), first)
                if not last:
                    x_transpose(b + 1, 2)
                main(b, 0, 0, range(HT, KT), first)
                if not last:
                    x_transpose(b + 1, 3)
                main(b, 0, 1, range(0, 1), first)
                if not last:
                    pe.wait_ge(s["xt_ready"], 4 * (b + 1) + 3)
                else:
                    pe.wait_ge(s["u_ready"], b)
                rank(b)
                main(b, 0, 1, range(1, 5), first)
                close(b, 0, 0)
                main(b, 0, 1, range(5, KT), first)
                close(b, 0, 1)
                for h in range(2):
                    main(b, 1, h, range(KT), first)
                    close(b, 1, h)

            pe.wait_ge(s["eff_set"], 2 * G)
            pe.wait_ge(s["w0_evac"], 2 * G)
            for i in range(4):
                x_transpose(0, i, first=True)
            pe.wait_ge(s["p_ready"], 3 * G)
            batch(0, first=True)
            with pe.Fori(1, NB - 1) as b:
                batch(b)
            batch(NB - 1, last=True)


_INS = ["x", "condB_coeff", "condB_codebook", "itok_B_0_23", "itok_B_4_50", "mask_Bx4096x4096_ik1", "L0_cond_W", "L0_cond_b",
        "L1_cond_weight", "L1_cond_scale_log", "L1_cond_lora_A", "L1_cond_lora_B", "L2_cond_W", "L2_cond_b",
        "L2_cond_lora_As", "L2_cond_lora_Bs", "L3_cond_A", "L3_cond_B"]


def kernel(**inputs):
    import numpy as np
    import concourse.bacc as bacc
    from concourse.bass_utils import run_bass_kernel_spmd as run

    nc = bacc.Bacc("TRN2", target_bir_lowering=False, num_devices=1)
    arrays, args = {}, []
    for name in _INS:
        a = np.ascontiguousarray(inputs[name])
        arrays[f"in_{name}"] = a
        args.append(nc.dram_tensor(f"in_{name}", a.shape, mybir.dt.from_np(a.dtype), kind="ExternalInput").ap())
    x = arrays["in_x"]
    out = nc.dram_tensor("out", x.shape, mybir.dt.from_np(x.dtype), kind="ExternalOutput").ap()
    cond_resid_chain(nc, *args, out)
    return run(nc, [arrays], core_ids=[0]).results[0]["out"]
```

```python
import concourse.bass as bass
from concourse import mybir
from contextlib import ExitStack

F32 = mybir.dt.float32
F32R = mybir.dt.float32r
I32 = mybir.dt.int32
U32 = mybir.dt.uint32
ALU = mybir.AluOpType
ACT = mybir.ActivationFunctionType
AXX = mybir.AxisListType.X


class Order:

    def __init__(self, engine, sem):
        self.engine, self.sem, self.base, self.n = engine, sem, 0, 0

    def did(self, ins):
        ins.then_inc(self.sem, 1)
        self.n += 1

    def wait(self):
        self.engine.wait_ge(self.sem, self.base + self.n)

    def rebase(self, base):
        self.base, self.n = base, 0


def cond_resid_chain(nc, x, coeff, codebook, tok2, tok3, mask, w0, b0, w1, scale_log, lora_a, lora_b,
                     w2, b2, a2, bb2, a3, bb3, out):
    NB, T, D = x.shape
    P = 128
    KT = D // P
    R = a2.shape[2]
    RL = lora_a.shape[0]
    NBR = NB * R
    TT = T // P
    HALF = D // 2
    HT = KT // 2
    NCB = codebook.shape[0]
    NTH = NCB - 1
    EXT = D + 2 * NBR
    G = KT
    MR = 4
    L1_SCALE, L2_SCALE = 0.5, 2.0

    w2_rows = w2.rearrange("(t p) n -> t p n", p=P)
    w1_cols = w1.rearrange("(h t p) (g c) -> h g p t c", p=P, h=2, c=P)
    w0_cols = w0.rearrange("(t p) (k c) -> k p t c", p=P, c=P)
    mask_rows = mask.rearrange("b (k p) n -> b k p n", p=P)
    x_rows = x.rearrange("b (t p) n -> b p t n", p=P)
    out_rows = out.rearrange("b (t p) (h n) -> b t h p n", p=P, h=2)
    a2_rows = a2.rearrange("s (t p) r -> s p t r", p=P)
    a3_rows = a3.rearrange("s (t p) r -> s p t r", p=P)

    w0t_dram = nc.dram_tensor("w0t_dram", [KT, P, D], F32, kind="Internal").ap()
    g_dram = nc.dram_tensor("g_dram", [NB, 2, 2, R, D], F32, kind="Internal").ap()
    y_dram = nc.dram_tensor("y_dram", [NB, R], F32, kind="Internal").ap()

    base = (nc.sbuf_base + 31) // 32 * 32
    names = {}

    def at(name, shape, dt, offset):
        return nc.alloc_sbuf_tensor_at(name, shape, dt, offset=offset)

    KB = 1024
    reg_p = base
    reg_ce = reg_p + 64 * KB
    reg_z1 = reg_ce + 16 * KB
    reg_ring = reg_z1 + 80 * KB
    reg_z3 = reg_ring + 16 * KB
    reg_la = reg_z3 + 21 * KB
    reg_b2 = reg_la + 4 * KB
    reg_c = reg_b2 + 4 * KB

    Ph = at("P_hi", [P, KT, D], F32R, reg_p)
    Pl = at("P_lo", [P, KT, D], F32R, reg_p + 32 * KB)
    Ceh = at("C_hi", [P, KT, 2, NB, R], F32R, reg_ce)
    Cel = at("C_lo", [P, KT, 2, NB, R], F32R, reg_ce + 8 * KB)
    w2n = at("w2_nat", [P, KT, D], F32, reg_p)
    lo = reg_p + 32 * KB
    b3n = at("b3_nat", [P, D], F32, lo)
    b3t = at("b3_t", [P, KT, NBR], F32, lo + 4 * KB)
    b2n = at("b2_nat", [P, D], F32, lo + 8 * KB)
    b2t = at("b2_t", [P, KT, NBR], F32, lo + 12 * KB)
    a3n = at("a3_nat", [P, KT, NB, R], F32, lo + 16 * KB)
    a3t = at("a3_t", [P, D], F32, lo + 20 * KB)
    a2n = at("a2_nat", [P, KT, NB, R], F32, lo + 24 * KB)
    lbn = at("lb_nat", [P, KT, RL], F32, lo + 28 * KB)
    own = at("own_batch", [P, NB, R], F32, reg_z3 + 20 * KB)
    b3b2 = at("b3_b2_t", [P, NBR], F32, reg_z3 + 20 * KB + 512)
    gah = at("ga_hi", [P, D], F32R, reg_ce)
    gal = at("ga_lo", [P, D], F32R, reg_ce + 4 * KB)
    a3h = at("a3_hi", [P, D], F32R, reg_ce + 8 * KB)
    a3l = at("a3_lo", [P, D], F32R, reg_ce + 12 * KB)
    Wh = at("w2_hi", [P, KT, EXT], F32R, reg_z1)
    Wl = at("w2_lo", [P, KT, EXT], F32R, reg_z1 + 40 * KB)
    w0t = at("w0_t", [P, KT, D], F32, reg_z1)
    Mh = at("m_hi", [P, MR, HALF], F32R, reg_z1 + 32 * KB)
    Ml = at("m_lo", [P, MR, HALF], F32R, reg_z1 + 40 * KB)
    xTh = at("x_t_hi", [P, KT, T], F32R, reg_z1 + 48 * KB)
    xTl = at("x_t_lo", [P, KT, T], F32R, reg_z1 + 56 * KB)
    x1h = at("x1_t_hi", [P, KT, T], F32R, reg_z1 + 64 * KB)
    x1l = at("x1_t_lo", [P, KT, T], F32R, reg_z1 + 72 * KB)
    ring_i = at("mask_ring", [P, MR, D], I32, reg_ring)
    ring_f = at("merged_ring", [P, MR, D], F32, reg_ring)
    pooled = at("pooled", [P, 2, HALF], F32, reg_ring)
    term_b = at("term_b", [P, HALF], F32, reg_ring + 4 * KB)
    term_c = at("term_c", [P, HALF], F32, reg_ring + 6 * KB)
    w0_out = at("w0_out", [P, D], F32, reg_ring + 8 * KB)
    w0n = at("w0_nat", [P, KT, P], F32, reg_ring + 12 * KB)
    raw = at("w1_raw", [P, 2, HT, P], F32, reg_z3)
    wn = at("w1_norm", [P, 2, HT, P], F32, reg_z3 + 4 * KB)
    term_a = at("term_a", [P, HALF], F32, lo + 28 * KB)
    term_d = at("term_d", [P, HALF], F32, lo + 30 * KB)
    W1h = at("w1_hi", [P, KT, P], F32R, reg_z3 + 8 * KB)
    W1l = at("w1_lo", [P, KT, P], F32R, reg_z3 + 12 * KB)
    acc = at("acc", [P, 2, HALF], F32, reg_z3 + 16 * KB)
    xn = at("x_nat", [P, TT, D], F32, reg_z3)
    Cb = at("c_batch", [P, KT, 4, 2, R], F32R, reg_z3 + 8 * KB)
    Gs = at("g_batch", [P, D], F32R, reg_z3 + 12 * KB)
    staged = at("out_staged", [P, 2, HALF], F32, reg_z3 + 16 * KB)
    Us = at("u_batch", [P, T], F32R, reg_z3 + 20 * KB)
    la = at("lora_a", [P, D], F32, reg_la)
    lbt = at("lora_b_t", [P, D], F32, reg_b2)
    b2all = at("b2_rows", [P, D], F32, reg_b2)

    off = [reg_c]

    def const(name, shape, dt=F32):
        n = 4
        for s in shape[1:]:
            n *= s
        t = at(name, shape, dt, off[0])
        off[0] += (n + 31) // 32 * 32
        return t

    ident = const("ident", [P, P])
    cb = const("codebook_rows", [P, NCB])
    cbn = const("codebook_neg", [P, NCB])
    mx = const("codebook_max", [P, 1])
    rmx = const("codebook_rmax", [P, 1])
    th = const("thresholds", [P, NTH])
    dd = const("steps", [P, NTH])
    cf = const("coeff_rows", [P, NB])
    now_tab = const("batch_cols", [P, NB, 3])
    now = const("batch_now", [P, 3])
    sc_now = const("scale_now", [P, KT])
    b0c = const("b0_cols", [P, KT])
    b2c = const("b2_cols", [P, KT])
    sc = const("scale", [P, KT, G])
    rs = const("scale_recip", [P, KT, G])
    rs_now = const("scale_recip_now", [P, KT])
    yc = const("y_col", [P, 1])
    tok = const("tokens", [P, 2, NB], I32)
    batch_off = const("batch_offset", [P, NB], I32)
    row_no = const("row_number", [P, 1], I32)
    slot_off = const("slot_offset", [P, 2, NB])
    slot_own = const("slot_own", [P, 2])
    rows = const("table_rows", [P, 2], U32)

    with ExitStack() as ctx:
        def sem(name):
            return ctx.enter_context(nc.semaphore(name))

        bank = [ctx.enter_context(nc.psum_tensor(f"bank{i}", [P, 512], F32)) for i in range(3)]
        dps = [ctx.enter_context(nc.psum_tensor(f"delta{i}", [P, D], F32)) for i in range(2)]
        bank += [dps[0][:, 0:512], dps[0][:, 512:1024], dps[1][:, 0:512], dps[1][:, 512:1024]]
        bank += [ctx.enter_context(nc.psum_tensor("bank7", [P, 512], F32))]

        s = {n: sem(n) for n in """small_in late_in lora_b_in lora_a_in w1_in0 w1_in1 a2_in b2_in a3_in b3_in w0_in w0_out_stored g_stored y_stored
            ub_in b2row_in x_in g_in recip_set tok_in b2c_in numbers_set rows_set ident_set ident_zero own_a own_b own_set ub_zero
            prep_done prep_hi prep_lo w2_eye ab_hi ab_lo b3b2_set y_set gsum_set scale_set cb_set coef_set ga_hi ga_lo
            delta_done raw_used eye_done rs_now_set normed terms pool_added scaled acc_ready eff_set w1_hi_set w1_ready
            p_used p_done p_hi p_ready w0_eye w0_tr w0_evac dve_step pool_step act_step
            s_set v_set h_set m_ready m_used l0_done x1_hi x1_ready t_done xt_hi xt_ready u_done u_hi u_ready c_ready
            out_done out_added out_st0 out_st1 lora_pad now_set scale_now""".split()}
        w2_in = [sem(f"w2_in{t}") for t in range(KT)]
        w0t_in = [sem(f"w0t_in{t}") for t in range(KT)]
        mask_in = [sem(f"mask_in{t}") for t in range(MR)]
        w1_in = [s["w1_in0"], s["w1_in1"]]
        out_stored = [s["out_st0"], s["out_st1"]]
        block = ctx.enter_context(nc.Block())

        LBT0 = 0
        W2_FIRST = 2
        B3T0 = 2 + 2 * W2_FIRST

        def w2_half(i):
            return 2 + i + 1 if i < 2 * W2_FIRST else 4 + i + 1

        V0 = 4 + 2 * KT
        B2T0 = V0 + 2
        B3B20 = B2T0 + 2
        A3T0 = B3B20 + 1
        GA0 = A3T0 + 2
        W2BANK = [0, 1, 2, 7]
        VBANK = [5, 6]
        HI_B3 = B3T0 + 2
        HI_V = V0
        HI_B2 = HI_V + 2
        HI_A3 = HI_B2 + 2

        @block.sync
        def _(sp):
            def row(v):
                return v.rearrange("(o n) -> o n", o=1)

            def raw_load(g, h):
                sp.dma_start(raw[:, h], w1_cols[h, g]).then_inc(w1_in[h], 16)

            sp.dma_start(lbn[:, :, :], lora_b.rearrange("(t p) r -> p t r", p=P)).then_inc(s["lora_b_in"], 16)
            sp.dma_start(la[0:RL, :], lora_a).then_inc(s["lora_a_in"], 16)
            sp.dma_start(sc[:, :, :], scale_log.rearrange("(t p) g o -> p t (g o)", p=P)).then_inc(s["small_in"], 16)
            sp.dma_start(cb[:, :], row(codebook).broadcast_to([P, NCB])).then_inc(s["small_in"], 16)
            for h in range(2):
                sp.dma_start(raw[:, h], w1_cols[h, 0]).then_inc(w1_in[h], 16)
            for t in range(KT):
                if t == W2_FIRST:
                    sp.wait_ge(s["rows_set"], 1)
                sp.dma_start(w2n[:, t], w2_rows[t]).then_inc(w2_in[t], 16)
            sp.dma_start(b2c[:, :], b2.rearrange("(t p) -> p t", p=P), allow_slow_non_contiguous=True).then_inc(s["b2c_in"], 16)
            with sp.Fori(0, NB) as b:
                slot = sp.value_load(row(tok2)[0:1, bass.ds(b, 1)], min_val=0, max_val=a2.shape[0] - 1)
                sp.dma_start(a2n[:, :, bass.ds(b, 1), :], a2_rows[bass.ds(slot, 1)].rearrange("s p t r -> p t s r")).then_inc(s["a2_in"], 16)
            sp.dma_start(w0n[:, :, :], w0_cols[0]).then_inc(s["w0_in"], 16)

            def raw_next(g, ahead, h):
                src = w1_cols[h, bass.ds(g + ahead, 1)].rearrange("g p t c -> (g p) t c")
                sp.wait_ge(s["raw_used"], 2 * g + 2 * ahead + h - 1)
                sp.dma_start(raw[:, h], src).then_inc(w1_in[h], 16)

            for h in range(2):
                raw_next(0, 1, h)
            sp.dma_start(cf[:, :], row(coeff).broadcast_to([P, NB])).then_inc(s["late_in"], 16)
            sp.dma_start(b0c[:, :], b0.rearrange("(t p) -> p t", p=P), allow_slow_non_contiguous=True).then_inc(s["late_in"], 16)
            sp.wait_ge(s["y_set"], 1)
            sp.dma_start(y_dram.rearrange("b (r o) -> (b r) o", o=1), yc[:, :]).then_inc(s["y_stored"], 16)
            for h in range(2):
                raw_next(0, 2, h)
            sp.wait_ge(s["y_stored"], 16)
            sp.wait_ge(s["ub_zero"], 1)
            for q in range(3):
                sp.dma_start(now_tab[q * 32 + R:q * 32 + 2 * R, :, 2], y_dram.rearrange("b r -> r b"), allow_slow_non_contiguous=True).then_inc(s["ub_in"], 16)
            sp.wait_ge(s["ga_hi"], 2)
            sp.wait_ge(s["ga_lo"], 2)
            for part, (ga, a3p) in enumerate(((gah, a3h), (gal, a3l))):
                sp.dma_start(g_dram[:, part, 0], ga[:, :].bitcast(F32)).then_inc(s["g_stored"], 16)
                sp.dma_start(g_dram[:, part, 1], a3p[:, :].bitcast(F32)).then_inc(s["g_stored"], 16)
            sp.wait_ge(s["g_stored"], 64)

            def group(g, load_w1, load_w0):
                if load_w1:
                    for h in range(2):
                        raw_next(g, 3, h)
                if load_w0:
                    src = w0_cols[bass.ds(g + 1, 1)].rearrange("k p t c -> (k p) t c")
                    sp.wait_ge(s["w0_tr"], 2 * g + 2)
                    sp.dma_start(w0n[:, :, :], src).then_inc(s["w0_in"], 16)
                sp.wait_ge(s["w0_evac"], 2 * (g + 1))
                sp.dma_start(w0t_dram[bass.ds(g, 1)].rearrange("k p n -> (k p) n"), w0_out[:, :]).then_inc(s["w0_out_stored"], 16)

            def load_x(b):
                sp.dma_start(xn[:, :, :], x_rows[b] if isinstance(b, int) else x_rows[bass.ds(b, 1)].rearrange("b p t n -> (b p) t n")).then_inc(s["x_in"], 16)

            def load_mask(b, k):
                src = mask_rows[b, k] if isinstance(b, int) else mask_rows[bass.ds(b, 1), k].rearrange("b p n -> (b p) n")
                sp.dma_start(ring_i[:, k % MR], src).then_inc(mask_in[k % MR], 16)

            def load_w0t(k):
                sp.wait_ge(s["p_used"], KT * (G - 1) + k + 1)
                sp.dma_start(w0t[:, k], w0t_dram[k]).then_inc(w0t_in[k], 16)

            with sp.Fori(0, G - 3) as g:
                group(g, True, True)
            group(G - 3, False, True)
            sp.wait_ge(s["terms"], 6 * 2 * G)
            load_x(0)
            group(G - 2, False, True)
            sp.wait_ge(s["eff_set"], 2 * G)
            load_mask(0, 0)
            load_mask(0, 1)
            sp.wait_ge(s["w0_out_stored"], 16 * (G - 1))
            before_last = 5
            for k in range(before_last):
                load_w0t(k)
            group(G - 1, False, False)
            for k in range(before_last, G - 1):
                load_w0t(k)
            sp.wait_ge(s["w0_out_stored"], 16 * G)
            load_mask(0, 2)
            load_mask(0, 3)
            load_w0t(KT - 1)

            def store(b, t):
                for h in range(2):
                    sp.wait_ge(s["out_added"], 4 * b + 2 * t + h + 1)
                    dst = out_rows[b, t, h] if isinstance(b, int) else out_rows[bass.ds(b, 1), t, h].rearrange("b p n -> (b p) n")
                    sp.dma_start(dst, staged[:, h]).then_inc(out_stored[h], 16)

            def batch(b, first=False, last=False):
                for k in range(MR, KT):
                    if k == MR + 2 and not first:
                        store(b - 1, 1)
                    sp.wait_ge(s["m_ready"], 2 * KT * b + 2 * (k - MR) + 2)
                    load_mask(b, k)
                if first:
                    sp.wait_ge(s["delta_done"], 2 * G)
                    sp.dma_start(b2all[:, :], row(b2).broadcast_to([P, D])).then_inc(s["b2row_in"], 16)
                    sp.wait_ge(s["p_used"], KT * G)
                else:
                    sp.wait_ge(s["out_done"], 4 * b)
                for part, rows in ((0, 0), (0, 32), (1, 64), (0, 96)):
                    src = g_dram[b, part] if isinstance(b, int) else g_dram[bass.ds(b, 1), part].rearrange("b s r n -> (b s) r n")
                    sp.dma_start(Gs[rows:rows + 32, :].bitcast(F32), src).then_inc(s["g_in"], 16)
                if not last:
                    sp.wait_ge(s["t_done"], 4 * (b + 1))
                    load_x(b + 1)
                    for k in range(MR):
                        sp.wait_ge(s["m_ready"], 2 * KT * b + 2 * (k + MR) + 2)
                        load_mask(b + 1, k)
                store(b, 0)

            batch(0, first=True)
            with sp.Fori(1, NB - 1) as b:
                batch(b)
            batch(NB - 1, last=True)
            store(NB - 1, 1)
            for h in range(2):
                sp.wait_ge(out_stored[h], 16 * 2 * NB)

        @block.gpsimd
        def _(pool):
            nc.gpsimd.memset(ident[:, :], 0.0).then_inc(s["ident_zero"], 1)
            nc.gpsimd.memset(own[:, :, :], 1.0).then_inc(s["own_a"], 1)
            pool.wait_ge(s["ident_zero"], 1)
            nc.gpsimd.affine_select(out=ident[:, :], in_=ident[:, :], compare_op=ALU.not_equal, fill=1.0, base=0,
                                    pattern=[[-1, P]], channel_multiplier=1).then_inc(s["ident_set"], 1)
            pool.wait_ge(s["own_a"], 1)
            nc.gpsimd.affine_select(out=own[:, :, :], in_=own[:, :, :], compare_op=ALU.is_ge, fill=0.0, base=0,
                                    pattern=[[-R, NB], [0, R]], channel_multiplier=1).then_inc(s["own_b"], 1)
            pool.wait_ge(s["own_b"], 1)
            nc.gpsimd.affine_select(out=own[:, :, :], in_=own[:, :, :], compare_op=ALU.is_ge, fill=0.0, base=R - 1,
                                    pattern=[[R, NB], [0, R]], channel_multiplier=-1).then_inc(s["own_set"], 1)
            nc.gpsimd.iota(batch_off[:, :], pattern=[[-R, NB]], base=0, channel_multiplier=0).then_inc(s["numbers_set"], 1)
            nc.gpsimd.iota(row_no[:, :], pattern=[[0, 1]], base=0, channel_multiplier=1).then_inc(s["numbers_set"], 1)
            pool.wait_ge(s["rows_set"], 1)
            nc.gpsimd.indirect_dma_start(b3n[:, :], None, bb3.rearrange("s r n -> (s r) n"),
                                         bass.IndirectOffsetOnAxis(rows[:, 1:2], 0)).then_inc(s["b3_in"], 16)
            nc.gpsimd.indirect_dma_start(b2n[:, :], None, bb2.rearrange("s r n -> (s r) n"),
                                         bass.IndirectOffsetOnAxis(rows[:, 0:1], 0)).then_inc(s["b2_in"], 16)
            step = Order(pool, s["pool_step"])

            def sums(q, h):
                n = 2 * q + h
                pl = pooled[:, h]
                for i, (count, part) in enumerate(((2, term_b[:, :]), (4, term_c[:, :]), (5, term_d[:, :]), (6, term_b[:, :]))):
                    pool.wait_ge(s["terms"], 6 * n + count)
                    if i:
                        step.wait()
                    step.did(nc.gpsimd.tensor_tensor(pl, pl, part, ALU.add))
                step.wait()
                nc.gpsimd.tensor_tensor(pl, pl, acc[:, h], ALU.add).then_inc(s["pool_added"], 1)

            def w0_diag(g):
                pool.wait_ge(s["w0_in"], 16 * g + 16)
                blk = w0n[:, bass.ds(g, 1), :].rearrange("p k c -> p (k c)")
                nc.gpsimd.tensor_tensor(blk, blk, ident[:, :], ALU.add).then_inc(s["w0_eye"], 1)

            def group(g, quant):
                if quant:
                    sums(g + 1, 1)
                if quant == 2:
                    sums(g + 2, 0)
                if quant:
                    w0_diag(g + 1)

            for h in range(2):
                sums(0, h)
            w0_diag(0)
            sums(1, 0)
            per = 2 * 2 * 4
            pairs = (G - 2) // 2
            start = step.n
            with pool.Fori(0, pairs) as j:
                step.rebase(start + j * per)
                group(2 * j, 2)
                group(2 * j + 1, 2)
                assert step.n == per
            step.rebase(start + pairs * per)
            group(G - 2, 1)

            def batch(b, first=False):
                if first:
                    pool.wait_ge(s["p_ready"], 3 * G)
                    pool.wait_ge(s["p_hi"], 3 * G)
                else:
                    pool.wait_ge(s["u_done"], b)
                for j in range(4):
                    src = (Ceh if j < 3 else Cel)[:, :, :, bass.ds(b, 1), :].rearrange("p k s b r -> p k s (b r)").bitcast(F32)
                    ins = nc.gpsimd.tensor_copy(Cb[:, :, j], src)
                    ins.then_inc(s["c_ready"], 1)

            batch(0, first=True)
            with pool.Fori(1, NB) as b:
                batch(b)

        @block.scalar
        def _(act):
            for i, v in enumerate((tok2, tok3)):
                act.dma_start(tok[:, i], v.rearrange("(o n) -> o n", o=1).broadcast_to([P, NB])).then_inc(s["tok_in"], 16)
            act.wait_ge(s["small_in"], 32)
            nc.scalar.activation(sc[:, :, :], sc[:, :, :], ACT.Exp).then_inc(s["scale_set"], 1)

            def scaled(q, h, first=False):
                if h == 0:
                    if not first:
                        act.wait_ge(s["scaled"], KT * q)
                        act.wait_ge(s["scale_set"], 1)
                    nc.scalar.copy(sc_now[:, :], sc[:, :, bass.ds(q, 1)].rearrange("p t g -> p (t g)")).then_inc(s["scale_now"], 1)
                    act.wait_ge(s["scale_now"], q + 1)
                act.wait_ge(s["pool_added"], 2 * q + h + 1)
                for t in range(HT):
                    blk = pooled[:, h, t * P:(t + 1) * P]
                    nc.scalar.activation(blk, blk, ACT.Copy, scale=sc_now[:, h * HT + t:h * HT + t + 1]).then_inc(s["scaled"], 1)

            def norm(q, h, first=False):
                if h == 0:
                    if not first:
                        act.wait_ge(s["normed"], KT * q)
                    else:
                        act.wait_ge(s["recip_set"], 1)
                    nc.scalar.copy(rs_now[:, :], rs[:, :, bass.ds(q, 1)].rearrange("p t g -> p (t g)")).then_inc(s["rs_now_set"], 1)
                    act.wait_ge(s["rs_now_set"], q + 1)
                act.wait_ge(s["raw_used"], 2 * q + h + 1)
                for t in range(HT):
                    blk = wn[:, h, t]
                    nc.scalar.activation(blk, blk, ACT.Copy, scale=rs_now[:, h * HT + t:h * HT + t + 1]).then_inc(s["normed"], 1)

            def w1_hi(q, h, first=False):
                act.wait_ge(s["eff_set"], 2 * q + h + 1)
                if not first:
                    act.wait_ge(s["p_used"], KT * (q - 1) + (h + 1) * HT)
                nc.scalar.copy(W1h[:, h * HT:(h + 1) * HT, :], acc[:, h]).then_inc(s["w1_hi_set"], 1)

            def p_hi(g, first=False):
                if first:
                    act.wait_ge(s["g_stored"], 64)
                for n in range(3):
                    if n < 2:
                        act.wait_ge(s["p_done"], 2 * g + n + 1)
                        dst = Ph[:, bass.ds(g, 1), n * 512:(n + 1) * 512].rearrange("p k n -> p (k n)")
                        nc.scalar.copy(dst, bank[n][:, :]).then_inc(s["p_hi"], 1)
                    else:
                        act.wait_ge(s["p_used"], KT * (g + 1))
                        dst = Ceh[:, bass.ds(g, 1)].rearrange("p k s b r -> p (k s b r)")
                        nc.scalar.copy(dst, bank[n][:, 0:2 * NBR]).then_inc(s["p_hi"], 1)

            def w0_evac(g, h, first=False):
                act.wait_ge(s["w0_tr"], 2 * g + h + 1)
                if not first:
                    act.wait_ge(s["w0_out_stored"], 16 * g)
                nc.scalar.copy(w0_out[:, h * 512:(h + 1) * 512], bank[7][:, :]).then_inc(s["w0_evac"], 1)

            for h in range(2):
                act.wait_ge(s["prep_done"], LBT0 + h + 1)
                nc.scalar.mul(lbt[0:RL, h * 512:(h + 1) * 512], bank[5 + h][0:RL, :], L1_SCALE).then_inc(s["prep_hi"], 1)
            def load_a3(b):
                slot = act.value_load(tok3.rearrange("(o n) -> o n", o=1)[0:1, b:b + 1], min_val=0, max_val=a3.shape[0] - 1)
                act.dma_start(a3n[:, :, b, :], a3_rows[bass.ds(slot, 1)].rearrange("s p t r -> (s p) t r")).then_inc(s["a3_in"], 16)

            for b in range(W2_FIRST):
                load_a3(b)
            act.wait_ge(s["scale_set"], 1)
            for h in range(2):
                norm(0, h, first=True)
            for t in range(KT):
                for h in range(2):
                    i = 2 * t + h
                    act.wait_ge(s["prep_done"], w2_half(i))
                    nc.scalar.copy(Wh[:, h * HT:(h + 1) * HT, t * P:(t + 1) * P], bank[W2BANK[i % 4]][:, :]).then_inc(s["prep_hi"], 1)
                if t == W2_FIRST - 1:
                    for h in range(2):
                        act.wait_ge(s["prep_done"], B3T0 + h + 1)
                        nc.scalar.copy(b3t[:, h * HT:(h + 1) * HT, :], bank[5 + h][:, :]).then_inc(s["prep_hi"], 1)
                elif t >= W2_FIRST:
                    load_a3(t)
                if t == HT:
                    scaled(0, 0, first=True)
            for h in range(2):
                act.wait_ge(s["prep_done"], V0 + h + 1)
                nc.scalar.copy(Wh[:, h * HT:(h + 1) * HT, D + NBR:EXT], bank[VBANK[h]][:, :]).then_inc(s["prep_hi"], 1)
            for h in range(2):
                act.wait_ge(s["prep_done"], B2T0 + h + 1)
                nc.scalar.copy(b2t[:, h * HT:(h + 1) * HT, :], bank[0 + h][:, :]).then_inc(s["prep_hi"], 1)
            scaled(0, 1, first=True)
            for h in range(2):
                w1_hi(0, h, first=True)
            for h in range(2):
                norm(1, h)
            for h in range(2):
                act.wait_ge(s["prep_done"], A3T0 + h + 1)
                nc.scalar.copy(a3t[:, h * 512:(h + 1) * 512], bank[h][:, :]).then_inc(s["prep_hi"], 1)
            act.wait_ge(s["a2_in"], 16 * NB)
            nc.scalar.copy(Wh[:, :, D:D + NBR], a2n[:, :, :, :]).then_inc(s["ab_hi"], 1)
            act.wait_ge(s["prep_hi"], HI_A3 + 2)
            nc.scalar.copy(a3h[:, :], a3t[:, :]).then_inc(s["ga_hi"], 1)
            act.wait_ge(s["gsum_set"], 2)
            nc.scalar.mul(gah[:, :], b2n[:, :], L2_SCALE).then_inc(s["ga_hi"], 1)

            def group(g, quant, first=False):
                if quant:
                    scaled(g + 1, 0)
                w0_evac(g, 0, first)
                if quant == 2:
                    norm(g + 2, 0)
                if quant:
                    w1_hi(g + 1, 0)
                if quant == 2:
                    norm(g + 2, 1)
                if quant:
                    scaled(g + 1, 1)
                w0_evac(g, 1, first)
                p_hi(g, first)
                if quant:
                    w1_hi(g + 1, 1)

            group(0, 2, first=True)
            group(1, 2)
            with act.Fori(1, (G - 2) // 2) as j:
                group(2 * j, 2)
                group(2 * j + 1, 2)
            group(G - 2, 1)

            def signs(b, k):
                act.wait_ge(mask_in[k % MR], 16 * (2 * b + k // MR + 1))
                nc.scalar.activation(ring_f[:, k % MR], ring_i[:, k % MR], ACT.Identity,
                                     bias=now[:, 1:2], scale=now[:, 0:1]).then_inc(s["s_set"], 1)

            def m_hi(b, k, first):
                act.wait_ge(s["v_set"], KT * b + k + 1)
                for h in range(2):
                    n = 2 * k + h
                    if not (first and n < MR):
                        act.wait_ge(s["m_used"], 2 * KT * b + n - MR + 1)
                    nc.scalar.copy(Mh[:, n % MR], ring_f[:, k % MR, h * HALF:(h + 1) * HALF]).then_inc(s["h_set"], 1)

            def x_hi(b, parts=range(4)):
                for i in parts:
                    act.wait_ge(s["t_done"], 4 * b + i + 1)
                    nc.scalar.copy(xTh[:, 2 * i:2 * i + 2, :], bank[6 + i % 2][:, :]).then_inc(s["xt_hi"], 1)

            def batch_now(b):
                nc.scalar.copy(now[:, :], now_tab[:, bass.ds(b, 1), :].rearrange("p b c -> p (b c)")).then_inc(s["now_set"], 1)
                act.wait_ge(s["now_set"], b + 1)

            act.wait_ge(s["coef_set"], 2)
            act.wait_ge(s["ub_in"], 48)
            batch_now(0)
            for h in range(2):
                w0_evac(G - 1, h)
                signs(0, h)
            act.wait_ge(s["p_used"], KT * (G - 1) + 5)
            x_hi(0, range(2))
            p_hi(G - 1)

            def batch(b, first=False, last=False):
                if not first:
                    act.wait_ge(s["u_ready"], b)
                    batch_now(b)
                    for k in range(2):
                        signs(b, k)
                for k in range(2):
                    m_hi(b, k, first)
                    if first and k == 0:
                        x_hi(0, range(2, 4))
                for k in range(2, MR if first else MR + 2):
                    signs(b, k)
                for k in range(2, KT):
                    m_hi(b, k, first)
                    if (first or k >= MR) and k + 2 < KT:
                        signs(b, k + 2)
                for o in range(KT):
                    if o % HT == 0:
                        act.wait_ge(s["l0_done"], 2 * b + o // HT + 1)
                    elif o % 2 == 0:
                        act.wait_ge(s["m_used"], 2 * KT * (b + 1) - 1 + o // HT)
                    nc.scalar.activation(x1h[:, o], bank[o // 2 if o // 2 < 4 else 0][:, (o % 2) * T:(o % 2 + 1) * T], ACT.Identity,
                                         bias=b0c[:, o:o + 1]).then_inc(s["x1_hi"], 1)
                if not last:
                    x_hi(b + 1)
                act.wait_ge(s["u_done"], b + 1)
                nc.scalar.activation(Us[:, :], bank[6][:, 0:T], ACT.Identity, bias=now[:, 2:3]).then_inc(s["u_hi"], 1)

            act.wait_ge(s["late_in"], 32)
            batch(0, first=True)
            with act.Fori(1, NB - 1) as b:
                batch(b)
            batch(NB - 1, last=True)

        @block.vector
        def _(dve):
            step = Order(dve, s["dve_step"])

            def link(ins):
                step.did(ins)
                step.wait()

            nc.vector.memset(now_tab[:, :, :], 0.0).then_inc(s["ub_zero"], 1)
            nc.vector.memset(la[RL:P, :], 0.0).then_inc(s["lora_pad"], 1)
            nc.vector.memset(lbt[RL:P, :], 0.0).then_inc(s["lora_pad"], 1)
            dve.wait_ge(s["tok_in"], 32)
            dve.wait_ge(s["numbers_set"], 2)
            for i in range(2):
                step.did(nc.vector.scalar_tensor_tensor(out=slot_off[:, i], in0=tok[:, i], scalar=float(R), in1=batch_off[:, :], op0=ALU.mult, op1=ALU.add))
            dve.wait_ge(s["own_set"], 1)
            step.wait()
            for i in range(2):
                step.did(nc.vector.tensor_tensor(slot_off[:, i], slot_off[:, i], own[:, :, 0], ALU.mult))
            step.wait()
            for i in range(2):
                step.did(nc.vector.reduce_sum(slot_own[:, i:i + 1], slot_off[:, i], AXX))
            step.wait()
            nc.vector.tensor_tensor(rows[:, :], slot_own[:, :], row_no[:, 0:1].broadcast_to([P, 2]), ALU.add).then_inc(s["rows_set"], 1)
            dve.wait_ge(s["small_in"], 32)
            link(nc.vector.tensor_scalar(cbn[:, :], cb[:, :], -1.0, None, ALU.mult))
            link(nc.vector.tensor_tensor(cbn[:, :], cbn[:, :], cb[:, :], ALU.max))
            link(nc.vector.reduce_max(mx[:, :], cbn[:, :], AXX))
            link(nc.vector.tensor_scalar(mx[:, :], mx[:, :], 1e-8, None, ALU.max))
            link(nc.vector.reciprocal(rmx[:, :], mx[:, :]))
            link(nc.vector.tensor_scalar(cb[:, :], cb[:, :], rmx[:, 0:1], None, ALU.mult))
            link(nc.vector.tensor_tensor(dd[:, :], cb[:, 1:NCB], cb[:, 0:NTH], ALU.subtract))
            link(nc.vector.tensor_tensor(th[:, :], cb[:, 1:NCB], cb[:, 0:NTH], ALU.add))
            link(nc.vector.tensor_scalar(th[:, :], th[:, :], 0.5, None, ALU.mult))

            def c(i):
                return th[:, i:i + 1]

            link(nc.vector.tensor_tensor(c(1), c(1), c(3), ALU.min))
            link(nc.vector.tensor_tensor(c(5), c(5), c(3), ALU.max))
            link(nc.vector.tensor_tensor(c(0), c(0), c(1), ALU.min))
            link(nc.vector.tensor_tensor(c(2), c(2), c(1), ALU.max))
            link(nc.vector.tensor_tensor(c(2), c(2), c(3), ALU.min))
            link(nc.vector.tensor_tensor(c(4), c(4), c(3), ALU.max))
            link(nc.vector.tensor_tensor(c(4), c(4), c(5), ALU.min))
            link(nc.vector.tensor_tensor(c(6), c(6), c(5), ALU.max))
            dve.wait_ge(s["scale_set"], 1)
            nc.vector.reciprocal(rs[:, :, :], sc[:, :, :]).then_inc(s["recip_set"], 1)
            def add_delta(q, h, par, first=False):
                n = 2 * q + h
                if not first:
                    dve.wait_ge(s["terms"], 6 * (n - 1))
                dve.wait_ge(w1_in[h], 16 * (q + 1))
                dve.wait_ge(s["delta_done"], n + 1)
                nc.vector.tensor_tensor(wn[:, h], raw[:, h], dps[par][:, h * 512:(h + 1) * 512], ALU.add).then_inc(s["raw_used"], 1)

            def terms(q, h, first=False, reused=True):
                n = 2 * q + h
                flat = wn[:, h].rearrange("p t c -> p (t c)")

                def term(i, dst):
                    return nc.vector.tensor_scalar(dst, flat, th[:, i:i + 1], dd[:, i:i + 1], ALU.is_gt, ALU.mult)

                dve.wait_ge(s["normed"], HT * (n + 1))
                if not first:
                    dve.wait_ge(s["terms"], 6 * n)
                if reused:
                    dve.wait_ge(s["w1_ready"], n - 1)
                step.did(term(0, acc[:, h]))
                step.did(term(1, term_a[:, :]))
                term(3, pooled[:, h]).then_inc(s["terms"], 1)
                if not first:
                    dve.wait_ge(s["pool_step"], 4 * n)
                term(4, term_b[:, :]).then_inc(s["terms"], 1)
                step.wait()
                nc.vector.scalar_tensor_tensor(out=acc[:, h], in0=acc[:, h], scalar=cb[:, 0:1], in1=term_a[:, :],
                                               op0=ALU.add, op1=ALU.add).then_inc(s["terms"], 1)
                term(5, term_c[:, :]).then_inc(s["terms"], 1)
                term(6, term_d[:, :]).then_inc(s["terms"], 1)
                dve.wait_ge(s["pool_step"], 4 * n + 1)
                term(2, term_b[:, :]).then_inc(s["terms"], 1)

            def effective(q, h, par):
                dve.wait_ge(s["scaled"], HT * (2 * q + h + 1))
                dve.wait_ge(s["eye_done"], q + 1)
                nc.vector.tensor_tensor(acc[:, h], pooled[:, h], dps[par][:, h * 512:(h + 1) * 512], ALU.add).then_inc(s["eff_set"], 1)

            def w1_lo(q, h):
                dve.wait_ge(s["w1_hi_set"], 2 * q + h + 1)
                nc.vector.tensor_tensor(W1l[:, h * HT:(h + 1) * HT, :], acc[:, h], W1h[:, h * HT:(h + 1) * HT, :].bitcast(F32),
                                        ALU.subtract).then_inc(s["w1_ready"], 1)

            def p_lo(g):
                for n in range(3):
                    dve.wait_ge(s["p_hi"], 3 * g + n + 1)
                    if n < 2:
                        cols = slice(n * 512, (n + 1) * 512)
                        hi = Ph[:, bass.ds(g, 1), cols].rearrange("p k n -> p (k n)").bitcast(F32)
                        lo_ = Pl[:, bass.ds(g, 1), cols].rearrange("p k n -> p (k n)")
                        nc.vector.tensor_tensor(lo_, bank[n][:, :], hi, ALU.subtract).then_inc(s["p_ready"], 1)
                    else:
                        hi = Ceh[:, bass.ds(g, 1)].rearrange("p k s b r -> p (k s b r)").bitcast(F32)
                        lo_ = Cel[:, bass.ds(g, 1)].rearrange("p k s b r -> p (k s b r)")
                        nc.vector.tensor_tensor(lo_, bank[n][:, 0:2 * NBR], hi, ALU.subtract).then_inc(s["p_ready"], 1)

            def w2_eye(t):
                dve.wait_ge(w2_in[t], 16)
                blk = w2n[:, t, t * P:(t + 1) * P]
                nc.vector.tensor_tensor(blk, blk, ident[:, :], ALU.add).then_inc(s["w2_eye"], 1)

            def w2_lo(t):
                for h in range(2):
                    i = 2 * t + h
                    dve.wait_ge(s["prep_hi"], w2_half(i))
                    dst = slice(h * HT, (h + 1) * HT), slice(t * P, (t + 1) * P)
                    nc.vector.tensor_tensor(Wl[:, dst[0], dst[1]], bank[W2BANK[i % 4]][:, :], Wh[:, dst[0], dst[1]].bitcast(F32),
                                            ALU.subtract).then_inc(s["prep_lo"], 1)

            dve.wait_ge(s["ident_set"], 1)
            w2_eye(0)
            for h in range(2):
                add_delta(0, h, 0, first=True)
            for t in range(1, 3):
                w2_eye(t)
            terms(0, 0, first=True, reused=False)
            for t in range(3, 6):
                w2_eye(t)
            for t in range(2):
                w2_lo(t)
            terms(0, 1, reused=False)
            for t in range(6, KT):
                w2_eye(t)
            for t in range(2, KT):
                w2_lo(t)
            for h in range(2):
                dve.wait_ge(s["prep_hi"], HI_V + h + 1)
                dst = Wl[:, h * HT:(h + 1) * HT, D + NBR:EXT]
                nc.vector.tensor_tensor(dst, bank[VBANK[h]][:, :], Wh[:, h * HT:(h + 1) * HT, D + NBR:EXT].bitcast(F32), ALU.subtract).then_inc(s["prep_lo"], 1)
            for h in range(2):
                effective(0, h, 0)
            for h in range(2):
                w1_lo(0, h)
            for h in range(2):
                add_delta(1, h, 1)
            dve.wait_ge(s["prep_done"], B3B20 + 1)
            nc.vector.tensor_tensor(b3b2[:, :], bank[2][:, 0:NBR], own[:, :, :].rearrange("p b r -> p (b r)"), ALU.mult).then_inc(s["b3b2_set"], 1)
            nc.vector.tensor_copy(yc[:, :], bank[2][:, NBR:NBR + 1]).then_inc(s["y_set"], 1)
            terms(1, 0)
            for h in range(2):
                dve.wait_ge(s["prep_done"], GA0 + h + 1)
                cols = slice(h * 512, (h + 1) * 512)
                nc.vector.tensor_tensor(b2n[:, cols], b2n[:, cols], bank[(2, 7)[h]][:, :], ALU.add).then_inc(s["gsum_set"], 1)
                if h == 0:
                    dve.wait_ge(s["ab_hi"], 1)
                    nc.vector.tensor_tensor(Wl[:, :, D:D + NBR], a2n[:, :, :, :].rearrange("p t b r -> p t (b r)"), Wh[:, :, D:D + NBR].bitcast(F32), ALU.subtract).then_inc(s["ab_lo"], 1)
            dve.wait_ge(s["ga_hi"], 1)
            nc.vector.tensor_tensor(a3l[:, :], a3t[:, :], a3h[:, :].bitcast(F32), ALU.subtract).then_inc(s["ga_lo"], 1)
            dve.wait_ge(s["ga_hi"], 2)
            nc.vector.scalar_tensor_tensor(out=gal[:, :], in0=b2n[:, :], scalar=L2_SCALE, in1=gah[:, :].bitcast(F32),
                                           op0=ALU.mult, op1=ALU.subtract).then_inc(s["ga_lo"], 1)

            def group(g, par, quant):
                if quant:
                    terms(g + 1, 1)
                if quant == 2:
                    add_delta(g + 2, 0, par)
                if quant:
                    effective(g + 1, 0, 1 - par)
                    w1_lo(g + 1, 0)
                if quant == 2:
                    add_delta(g + 2, 1, par)
                    terms(g + 2, 0)
                if quant:
                    effective(g + 1, 1, 1 - par)
                p_lo(g)
                if quant:
                    w1_lo(g + 1, 1)

            per = 2 * 2 * 2
            pairs = (G - 2) // 2
            start = step.n
            with dve.Fori(0, pairs) as j:
                step.rebase(start + j * per)
                group(2 * j, 0, 2)
                group(2 * j + 1, 1, 2)
                assert step.n == per, step.n
            step.rebase(start + pairs * per)
            dve.wait_ge(s["late_in"], 32)
            nc.vector.tensor_scalar(now_tab[:, :, 0], cf[:, :], 2.0, None, ALU.mult).then_inc(s["coef_set"], 1)
            nc.vector.tensor_scalar(now_tab[:, :, 1], cf[:, :], -1.0, None, ALU.mult).then_inc(s["coef_set"], 1)

            group(G - 2, 0, 1)

            def merged(b, k, first):
                if first:
                    dve.wait_ge(w0t_in[k], 16)
                dve.wait_ge(s["s_set"], KT * b + k + 1)
                nc.vector.tensor_tensor(ring_f[:, k % MR], ring_f[:, k % MR], w0t[:, k], ALU.add).then_inc(s["v_set"], 1)

            def m_lo(b, k):
                for h in range(2):
                    n = 2 * k + h
                    dve.wait_ge(s["h_set"], 2 * KT * b + n + 1)
                    nc.vector.tensor_tensor(Ml[:, n % MR], ring_f[:, k % MR, h * HALF:(h + 1) * HALF], Mh[:, n % MR].bitcast(F32),
                                            ALU.subtract).then_inc(s["m_ready"], 1)

            def x_lo(b, parts=range(4)):
                for i in parts:
                    dve.wait_ge(s["xt_hi"], 4 * b + i + 1)
                    nc.vector.tensor_tensor(xTl[:, 2 * i:2 * i + 2, :], bank[6 + i % 2][:, :], xTh[:, 2 * i:2 * i + 2, :].bitcast(F32),
                                            ALU.subtract).then_inc(s["xt_ready"], 1)

            for k in range(2):
                merged(0, k, True)
            dve.wait_ge(s["p_used"], KT * (G - 1) + 5)
            x_lo(0, range(2))
            p_lo(G - 1)

            def out_add(b, t, first=False):
                for h in range(2):
                    if first and h == 0:
                        dve.wait_ge(s["b2row_in"], 16)
                    dve.wait_ge(s["out_done"], 4 * b + 2 * t + h + 1)
                    if not first:
                        dve.wait_ge(out_stored[h], 16 * (2 * b + t))
                    nc.vector.tensor_tensor(staged[:, h], bank[4 + h][:, :], b2all[:, h * HALF:(h + 1) * HALF], ALU.add).then_inc(s["out_added"], 1)

            def batch(b, first=False, last=False):
                if not first:
                    for k in range(2):
                        merged(b, k, first)
                for k in range(2):
                    m_lo(b, k)
                    if first and k == 0:
                        x_lo(0, range(2, 4))
                for k in range(2, MR if first else MR + 2):
                    merged(b, k, first)
                if not first:
                    out_add(b - 1, 1)
                for k in range(2, KT):
                    m_lo(b, k)
                    if (first or k >= MR) and k + 2 < KT:
                        merged(b, k + 2, first)
                for o in range(KT):
                    if o % 2 == 0:
                        dve.wait_ge(s["x1_hi"], KT * b + o + 2)
                    nc.vector.scalar_tensor_tensor(out=x1l[:, o], in0=bank[o // 2][:, (o % 2) * T:(o % 2 + 1) * T], scalar=b0c[:, o:o + 1],
                                                   in1=x1h[:, o].bitcast(F32), op0=ALU.add, op1=ALU.subtract).then_inc(s["x1_ready"], 1)
                if not last:
                    x_lo(b + 1)
                dve.wait_ge(s["u_hi"], b + 1)
                rows = slice(32, 64)
                nc.vector.scalar_tensor_tensor(out=Us[rows, :], in0=bank[6][rows, 0:T], scalar=now[rows, 2:3],
                                               in1=Us[rows, :].bitcast(F32), op0=ALU.add, op1=ALU.subtract).then_inc(s["u_ready"], 1)
                out_add(b, 0, first)

            batch(0, first=True)
            with dve.Fori(1, NB - 1) as b:
                batch(b)
            batch(NB - 1, last=True)
            out_add(NB - 1, 1)

        @block.tensor
        def _(pe):
            mm = nc.tensor.matmul

            pe.wait_ge(s["ident_set"], 1)
            pe.wait_ge(s["lora_b_in"], 16)
            for h in range(2):
                for t in range(HT):
                    ins = nc.tensor.transpose(bank[5 + h][0:RL, t * P:(t + 1) * P], lbn[:, h * HT + t, :], ident[:, :])
                ins.then_inc(s["prep_done"], 1)

            def delta(q, par, first=False):
                for h in range(2):
                    pe.wait_ge(s["prep_hi"], 2)
                    if not first:
                        pe.wait_ge(s["eff_set"], 2 * (q - 2) + h + 1)
                    for t in range(HT):
                        k = h * HT + t
                        ins = mm(dps[par][:, k * P:(k + 1) * P], lbt[:, k * P:(k + 1) * P], la[:, bass.ds(q * P, P)],
                                 start=(t == 0), stop=True, skip_group_check=True)
                    ins.then_inc(s["delta_done"], 1)

            def eye(q, par):
                pe.wait_ge(s["raw_used"], 2 * (q + 1))
                mm(dps[par][:, bass.ds(q * P, P)], ident[:, :], ident[:, :], start=False, stop=True, skip_group_check=True).then_inc(s["eye_done"], 1)

            def w0_transpose(g, h, first=False):
                if h == 0:
                    pe.wait_ge(s["w0_eye"], g + 1)
                if not (first and h == 0):
                    pe.wait_ge(s["w0_evac"], 2 * g + h)
                for j in range(HT):
                    ins = nc.tensor.transpose(bank[7][:, j * P:(j + 1) * P], w0n[:, h * HT + j, :], ident[:, :])
                ins.then_inc(s["w0_tr"], 1)

            pe.wait_ge(s["lora_pad"], 2)
            pe.wait_ge(s["lora_a_in"], 16)
            delta(0, 0, first=True)
            def w2_transpose(t):
                pe.wait_ge(s["w2_eye"], t + 1)
                for h in range(2):
                    i = 2 * t + h
                    if i >= 4:
                        pe.wait_ge(s["prep_lo"], i - 3)
                    for j in range(HT):
                        k = h * HT + j
                        ins = nc.tensor.transpose(bank[W2BANK[i % 4]][:, j * P:(j + 1) * P], w2n[:, t, k * P:(k + 1) * P], ident[:, :])
                    ins.then_inc(s["prep_done"], 1)

            def v_part(t):
                for h in range(2):
                    for j in range(HT):
                        k = h * HT + j
                        ins = mm(bank[VBANK[h]][:, j * P:(j + 1) * P], w2n[:, t, k * P:(k + 1) * P], b3t[:, t],
                                 start=(t == 0 and j == 0), stop=(t == KT - 1), skip_group_check=True)
                    if t == KT - 1:
                        ins.then_inc(s["prep_done"], 1)

            for t in range(W2_FIRST):
                w2_transpose(t)
            pe.wait_ge(s["b3_in"], 16)
            for h in range(2):
                for t in range(HT):
                    k = h * HT + t
                    ins = nc.tensor.transpose(bank[5 + h][:, t * P:(t + 1) * P], b3n[:, k * P:(k + 1) * P], ident[:, :])
                ins.then_inc(s["prep_done"], 1)
            eye(0, 0)
            pe.wait_ge(s["prep_hi"], HI_B3)
            for t in range(W2_FIRST):
                v_part(t)
            for t in range(W2_FIRST, KT):
                w2_transpose(t)
                v_part(t)
            pe.wait_ge(s["b2_in"], 16)
            pe.wait_ge(s["prep_lo"], 2 * KT)
            for h in range(2):
                for t in range(HT):
                    k = h * HT + t
                    ins = nc.tensor.transpose(bank[h][:, t * P:(t + 1) * P], b2n[:, k * P:(k + 1) * P], ident[:, :])
                ins.then_inc(s["prep_done"], 1)
            pe.wait_ge(s["prep_lo"], 2 * KT + 2)
            delta(1, 1, first=True)
            pe.wait_ge(s["prep_hi"], HI_B2 + 2)
            pe.wait_ge(s["b2c_in"], 16)
            for k in range(KT):
                mm(bank[2][:, 0:NBR], b3t[:, k], b2t[:, k], start=(k == 0), stop=(k == KT - 1), skip_group_check=True)
                ins = mm(bank[2][:, NBR:NBR + 1], b3t[:, k], b2c[:, k:k + 1], start=False, stop=(k == KT - 1), skip_group_check=True)
            ins.then_inc(s["prep_done"], 1)
            pe.wait_ge(s["a3_in"], 16 * NB)
            for h in range(2):
                for t in range(HT):
                    ins = nc.tensor.transpose(bank[h][:, t * P:(t + 1) * P], a3n[:, h * HT + t].rearrange("p b r -> p (b r)"), ident[:, :])
                ins.then_inc(s["prep_done"], 1)
            pe.wait_ge(s["b3b2_set"], 1)
            pe.wait_ge(s["y_set"], 1)
            pe.wait_ge(s["prep_hi"], HI_A3 + 2)
            for h in range(2):
                mm(bank[(2, 7)[h]][:, :], b3b2[:, :], a3t[:, h * 512:(h + 1) * 512], start=True, stop=True).then_inc(s["prep_done"], 1)

            def x_transpose(b, i):
                if i == 0:
                    pe.wait_ge(s["x_in"], 16 * (b + 1))
                if i >= 2:
                    pe.wait_ge(s["xt_ready"], 4 * b + i - 1)
                for j in range(2):
                    for t in range(TT):
                        k = 2 * i + j
                        c0 = j * T + t * P
                        ins = nc.tensor.transpose(bank[6 + i % 2][:, c0:c0 + P], xn[:, t, k * P:(k + 1) * P], ident[:, :])
                ins.then_inc(s["t_done"], 1)

            COLS = [(0, 512), (512, 1024), (1024, EXT)]

            def group(g, par, quant, first=False, last=False):
                if quant:
                    eye(g + 1, 1 - par)
                if quant == 2:
                    delta(g + 2, par)
                if first:
                    pe.wait_ge(s["prep_lo"], 2 * KT + 2)
                for t in range(KT):
                    if t % HT == 0:
                        pe.wait_ge(s["w1_ready"], 2 * g + t // HT + 1)
                    if t in (2, 5):
                        if first and t == 2:
                            pe.wait_ge(s["gsum_set"], 2)
                        w0_transpose(g, t // HT, first)
                    if last and t >= 6:
                        pe.wait_ge(s["eff_set"], 2 * G)
                        if t == 7:
                            pe.wait_ge(s["w0_evac"], 2 * G)
                        x_transpose(0, t - 6)
                    for n, (c0, c1) in enumerate(COLS):
                        if t == 0 and first and n == 2:
                            pe.wait_ge(s["gsum_set"], 1)
                            pe.wait_ge(s["ab_lo"], 1)
                        if t == 0 and not first:
                            pe.wait_ge(s["p_ready"], 3 * (g - 1) + n + 1)
                        o = bank[n][:, 0:c1 - c0]
                        mm(o, W1h[:, t], Wh[:, t, c0:c1], start=(t == 0), stop=False)
                        mm(o, W1h[:, t], Wl[:, t, c0:c1], start=False, stop=False)
                        ins = mm(o, W1l[:, t], Wh[:, t, c0:c1], start=False, stop=(t == KT - 1))
                        if n == 2:
                            ins.then_inc(s["p_used"], 1)
                        elif t == KT - 1:
                            ins.then_inc(s["p_done"], 1)

            group(0, 0, 2, first=True)
            group(1, 1, 2)
            with pe.Fori(1, (G - 2) // 2) as j:
                group(2 * j, 0, 2)
                group(2 * j + 1, 1, 2)
            group(G - 2, 0, 1)
            group(G - 1, 1, 0, last=True)

            def layer0(b, first=False):
                for k in range(KT):
                    for o in range(KT):
                        h = o // HT
                        n = 2 * k + h
                        if o % HT == 0:
                            pe.wait_ge(s["m_ready"], 2 * KT * b + n + 1)
                        if k == 0 and o % 2 == 0 and not first:
                            pe.wait_ge(s["x1_ready"], KT * (b - 1) + o + 2)
                        if first and k % 2 == 0 and o == 0:
                            pe.wait_ge(s["xt_ready"], k // 2 + 1)
                        if not first and k == 0 and o == 0:
                            pe.wait_ge(s["xt_ready"], 4 * (b + 1))
                        dst = bank[o // 2][:, (o % 2) * T:(o % 2 + 1) * T]
                        cols = slice((o % HT) * P, (o % HT + 1) * P)
                        mh, ml = Mh[:, n % MR, cols], Ml[:, n % MR, cols]
                        mm(dst, mh, xTh[:, k], start=(k == 0 and o % 2 == 0), stop=False, skip_group_check=True)
                        mm(dst, mh, xTl[:, k], start=False, stop=False, skip_group_check=True)
                        ins = mm(dst, ml, xTh[:, k], start=False, stop=(k == KT - 1), skip_group_check=True)
                        if o % HT == HT - 1:
                            ins.then_inc(s["m_used"], 1)
                        elif k == KT - 1 and o % 2 == 1:
                            ins.then_inc(s["l0_done"], 1)

            def main(b, t, h, ks, first=False):
                o = bank[4 + h][:, :]
                toks = slice(t * P, (t + 1) * P)
                cols = slice(h * HALF, (h + 1) * HALF)
                for k in ks:
                    if k == 0 and not (first and t == 0):
                        pe.wait_ge(s["out_added"], 4 * b + 2 * t + h - 1)
                    if t == 0 and h == 0:
                        pe.wait_ge(s["x1_ready"], KT * b + k + 1)
                    mm(o, x1h[:, k, toks], Ph[:, k, cols], start=(k == 0), stop=False)
                    mm(o, x1h[:, k, toks], Pl[:, k, cols], start=False, stop=False)
                    mm(o, x1l[:, k, toks], Ph[:, k, cols], start=False, stop=False)

            def rank(b):
                pe.wait_ge(s["c_ready"], 4 * (b + 1))
                for k in range(KT):
                    ck = Cb[:, k].rearrange("p j s r -> p (j s r)")
                    mm(bank[6][:, 0:T], ck, x1h[:, k], start=(k == 0), stop=False)
                    ins = mm(bank[6][:, 0:T], ck, x1l[:, k], start=False, stop=(k == KT - 1))
                ins.then_inc(s["u_done"], 1)

            def close(b, t, h):
                if t == 0 and h == 0:
                    pe.wait_ge(s["u_ready"], b + 1)
                    pe.wait_ge(s["g_in"], 64 * (b + 1))
                mm(bank[4 + h][:, :], Us[:, t * P:(t + 1) * P], Gs[:, h * HALF:(h + 1) * HALF], start=False, stop=True).then_inc(s["out_done"], 1)

            def batch(b, first=False, last=False):
                layer0(b, first)
                if not last:
                    if first:
                        pe.wait_ge(s["xt_ready"], 4)
                    else:
                        pe.wait_ge(s["u_ready"], b)
                    x_transpose(b + 1, 0)
                    pe.wait_ge(s["xt_ready"], 4 * (b + 1))
                    x_transpose(b + 1, 1)
                main(b, 0, 0, range(0, HT), first)
                if not last:
                    x_transpose(b + 1, 2)
                main(b, 0, 0, range(HT, KT), first)
                if not last:
                    x_transpose(b + 1, 3)
                main(b, 0, 1, range(0, 1), first)
                if not last:
                    pe.wait_ge(s["xt_ready"], 4 * (b + 1) + 3)
                else:
                    pe.wait_ge(s["u_ready"], b)
                rank(b)
                main(b, 0, 1, range(1, 5), first)
                close(b, 0, 0)
                main(b, 0, 1, range(5, KT), first)
                close(b, 0, 1)
                for h in range(2):
                    main(b, 1, h, range(KT), first)
                    close(b, 1, h)

            for i in range(2, 4):
                x_transpose(0, i)
            pe.wait_ge(s["p_ready"], 3 * G)
            batch(0, first=True)
            with pe.Fori(1, NB - 1) as b:
                batch(b)
            batch(NB - 1, last=True)


_INS = ["x", "condB_coeff", "condB_codebook", "itok_B_0_23", "itok_B_4_50", "mask_Bx4096x4096_ik1", "L0_cond_W", "L0_cond_b",
        "L1_cond_weight", "L1_cond_scale_log", "L1_cond_lora_A", "L1_cond_lora_B", "L2_cond_W", "L2_cond_b",
        "L2_cond_lora_As", "L2_cond_lora_Bs", "L3_cond_A", "L3_cond_B"]


def kernel(**inputs):
    import numpy as np
    import concourse.bacc as bacc
    from concourse.bass_utils import run_bass_kernel_spmd as run

    nc = bacc.Bacc("TRN2", target_bir_lowering=False, num_devices=1)
    arrays, args = {}, []
    for name in _INS:
        a = np.ascontiguousarray(inputs[name])
        arrays[f"in_{name}"] = a
        args.append(nc.dram_tensor(f"in_{name}", a.shape, mybir.dt.from_np(a.dtype), kind="ExternalInput").ap())
    x = arrays["in_x"]
    out = nc.dram_tensor("out", x.shape, mybir.dt.from_np(x.dtype), kind="ExternalOutput").ap()
    cond_resid_chain(nc, *args, out)
    return run(nc, [arrays], core_ids=[0]).results[0]["out"]
```
